# Optimizing a Trainium2 kernel written in Bass

```python
import numpy as np
import jax
import jax.numpy as jnp

def _softmax(x, axis=-1):
    return jax.nn.softmax(x, axis=axis)

def _gelu(x):
    return jax.nn.gelu(x, approximate=True)

def _silu(x):
    return jax.nn.silu(x)

def _sigmoid(x):
    return jax.nn.sigmoid(x)

def _layernorm(x, axis=-1, eps=1e-05):
    m = jnp.mean(x, axis=axis, keepdims=True)
    v = jnp.var(x, axis=axis, keepdims=True)
    return (x - m) / jnp.sqrt(v + eps)

def _scatter_add(tgt, idx, src, axis=0):
    return tgt.at[idx].add(src)

def _segment_sum(src, seg, n):
    return jax.ops.segment_sum(src, seg, n)
kernel_name = 'mk_conv_preact_d4_conv_nchw128_r2_f963cf'

def setup_inputs(seed: int=0):
    np.random.seed(seed)
    _w = jnp.asarray

    def _rec_inputs():
        import jax
        import jax.numpy as jnp
        _gk = jax.random.key(seed)
        x = -0.000125 + 0.9999 * jax.random.normal(jax.random.fold_in(_gk, 1), (16, 64, 64, 64), jnp.float32)
        return x
    x = _rec_inputs()

    def _L0_conv_setup():
        import jax, jax.numpy as jnp
        import numpy as np
        STRIDE = 1
        PADDING = 1
        key = jax.random.key(seed)
        ks = jax.random.split(key, 5)
        B, C_in, C_out, K, KS, H, W, HID = (16, 64, 64, 4, 3, 64, 64, 32)
        return {'x': jax.random.normal(ks[0], (B, C_in, H, W), dtype=jnp.float32), 'experts': jax.random.normal(ks[1], (K, C_out, C_in, KS, KS), dtype=jnp.float32) * 0.02, 'bias': jnp.zeros((K, C_out), dtype=jnp.float32), 'w1': jax.random.normal(ks[2], (HID, C_in), dtype=jnp.float32) * 0.05, 'b1': jnp.zeros((HID,), dtype=jnp.float32), 'w2': jax.random.normal(ks[3], (K, HID), dtype=jnp.float32) * 0.05, 'b2': jnp.zeros((K,), dtype=jnp.float32)}
    _L0_conv_all = _L0_conv_setup()
    _L0_conv_in = {k: v for k, v in _L0_conv_all.items() if k in ('experts', 'bias', 'w1', 'b1', 'w2', 'b2')}
    del _L0_conv_all

    def _L1_conv_setup():
        import jax, jax.numpy as jnp
        import numpy as np
        import math
        C = 64
        KSIZE = 9
        PAD = KSIZE // 2

        def _conv1d(v, w, b):
            y = jax.lax.conv_general_dilated(v, w, window_strides=(1,), padding=[(PAD, PAD)], dimension_numbers=('NCH', 'OIH', 'NCH'))
            return y + b[None, :, None]

        def _sweep(x, w, b, axis, reverse):
            rows = jnp.moveaxis(x, axis, 0)
            if reverse:
                rows = rows[::-1]

            def step(prev, row):
                new = row + jax.nn.relu(_conv1d(prev, w, b))
                return (new, new)
            _, rest = jax.lax.scan(step, rows[0], rows[1:])
            out = jnp.concatenate([rows[:1], rest], axis=0)
            if reverse:
                out = out[::-1]
            return jnp.moveaxis(out, 0, axis)
        key = jax.random.key(seed)
        ks = jax.random.split(key, 9)
        B, H, W = (32, 36, 100)
        bound = math.sqrt(2.0 / (C * 9 * 5))
        x = jax.random.normal(ks[0], (B, C, H, W), dtype=jnp.float32)

        def wgt(k):
            return jax.random.uniform(k, (C, C, KSIZE), dtype=jnp.float32, minval=-bound, maxval=bound)

        def bia(k):
            return 0.01 * jax.random.normal(k, (C,), dtype=jnp.float32)
        return {'x': x, 'w_d': wgt(ks[1]), 'b_d': bia(ks[2]), 'w_u': wgt(ks[3]), 'b_u': bia(ks[4]), 'w_r': wgt(ks[5]), 'b_r': bia(ks[6]), 'w_l': wgt(ks[7]), 'b_l': bia(ks[8])}
    _L1_conv_all = _L1_conv_setup()
    _L1_conv_in = {k: v for k, v in _L1_conv_all.items() if k in ('w_d', 'b_d', 'w_u', 'b_u', 'w_r', 'b_r', 'w_l', 'b_l')}
    del _L1_conv_all

    def _L2_conv_setup():
        import jax, jax.numpy as jnp
        import numpy as np
        from jax import lax
        BASE = 10000.0

        def _rope(x):
            b, h, w, c = x.shape
            k_max = c // 2
            theta = 1.0 / BASE ** (jnp.arange(k_max, dtype=x.dtype) / k_max)
            angles = jnp.arange(h, dtype=x.dtype)[:, None] * theta
            cos = jnp.cos(angles)[None, None]
            sin = jnp.sin(angles)[None, None]
            xr = x.reshape(b, h, w, k_max, 2)
            re, im = (xr[..., 0], xr[..., 1])
            out = jnp.stack([re * cos - im * sin, re * sin + im * cos], axis=-1)
            return out.reshape(b, h, w, c)
        key = jax.random.key(seed)
        k1, k2, k3 = jax.random.split(key, 3)
        B, C, H, W = (8, 64, 80, 80)
        x = jax.random.normal(k1, (B, C, H, W), dtype=jnp.float32)
        qk_w = jax.random.normal(k2, (2 * C, C), dtype=jnp.float32) * 0.02
        qk_b = jnp.zeros((2 * C,), dtype=jnp.float32)
        lepe_w = jax.random.normal(k3, (C, 1, 3, 3), dtype=jnp.float32) * 0.1
        lepe_b = jnp.zeros((C,), dtype=jnp.float32)
        return {'x': x, 'qk_w': qk_w, 'qk_b': qk_b, 'lepe_w': lepe_w, 'lepe_b': lepe_b, 'num_heads': 8}
    _L2_conv_all = _L2_conv_setup()
    _L2_conv_in = {k: v for k, v in _L2_conv_all.items() if k in ('qk_w', 'qk_b', 'lepe_w', 'lepe_b')}
    del _L2_conv_all

    def _L3_conv_setup():
        import jax, jax.numpy as jnp
        import numpy as np
        import math
        C = 64
        KSIZE = 9
        PAD = KSIZE // 2

        def _conv1d(v, w, b):
            y = jax.lax.conv_general_dilated(v, w, window_strides=(1,), padding=[(PAD, PAD)], dimension_numbers=('NCH', 'OIH', 'NCH'))
            return y + b[None, :, None]

        def _sweep(x, w, b, axis, reverse):
            rows = jnp.moveaxis(x, axis, 0)
            if reverse:
                rows = rows[::-1]

            def step(prev, row):
                new = row + jax.nn.relu(_conv1d(prev, w, b))
                return (new, new)
            _, rest = jax.lax.scan(step, rows[0], rows[1:])
            out = jnp.concatenate([rows[:1], rest], axis=0)
            if reverse:
                out = out[::-1]
            return jnp.moveaxis(out, 0, axis)
        key = jax.random.key(seed)
        ks = jax.random.split(key, 9)
        B, H, W = (32, 36, 100)
        bound = math.sqrt(2.0 / (C * 9 * 5))
        x = jax.random.normal(ks[0], (B, C, H, W), dtype=jnp.float32)

        def wgt(k):
            return jax.random.uniform(k, (C, C, KSIZE), dtype=jnp.float32, minval=-bound, maxval=bound)

        def bia(k):
            return 0.01 * jax.random.normal(k, (C,), dtype=jnp.float32)
        return {'x': x, 'w_d': wgt(ks[1]), 'b_d': bia(ks[2]), 'w_u': wgt(ks[3]), 'b_u': bia(ks[4]), 'w_r': wgt(ks[5]), 'b_r': bia(ks[6]), 'w_l': wgt(ks[7]), 'b_l': bia(ks[8])}
    _L3_conv_all = _L3_conv_setup()
    _L3_conv_in = {k: v for k, v in _L3_conv_all.items() if k in ('w_d', 'b_d', 'w_u', 'b_u', 'w_r', 'b_r', 'w_l', 'b_l')}
    del _L3_conv_all
    return {'x': x, 'L0_conv_experts': _L0_conv_in['experts'], 'L0_conv_bias': _L0_conv_in['bias'], 'L0_conv_w1': _L0_conv_in['w1'], 'L0_conv_b1': _L0_conv_in['b1'], 'L0_conv_w2': _L0_conv_in['w2'], 'L0_conv_b2': _L0_conv_in['b2'], 'L1_conv_w_d': _L1_conv_in['w_d'], 'L1_conv_b_d': _L1_conv_in['b_d'], 'L1_conv_w_u': _L1_conv_in['w_u'], 'L1_conv_b_u': _L1_conv_in['b_u'], 'L1_conv_w_r': _L1_conv_in['w_r'], 'L1_conv_b_r': _L1_conv_in['b_r'], 'L1_conv_w_l': _L1_conv_in['w_l'], 'L1_conv_b_l': _L1_conv_in['b_l'], 'L2_conv_qk_w': _L2_conv_in['qk_w'], 'L2_conv_qk_b': _L2_conv_in['qk_b'], 'L2_conv_lepe_w': _L2_conv_in['lepe_w'], 'L2_conv_lepe_b': _L2_conv_in['lepe_b'], 'L3_conv_w_d': _L3_conv_in['w_d'], 'L3_conv_b_d': _L3_conv_in['b_d'], 'L3_conv_w_u': _L3_conv_in['w_u'], 'L3_conv_b_u': _L3_conv_in['b_u'], 'L3_conv_w_r': _L3_conv_in['w_r'], 'L3_conv_b_r': _L3_conv_in['b_r'], 'L3_conv_w_l': _L3_conv_in['w_l'], 'L3_conv_b_l': _L3_conv_in['b_l']}

def reference(x, L0_conv_experts, L0_conv_bias, L0_conv_w1, L0_conv_b1, L0_conv_w2, L0_conv_b2, L1_conv_w_d, L1_conv_b_d, L1_conv_w_u, L1_conv_b_u, L1_conv_w_r, L1_conv_b_r, L1_conv_w_l, L1_conv_b_l, L2_conv_qk_w, L2_conv_qk_b, L2_conv_lepe_w, L2_conv_lepe_b, L3_conv_w_d, L3_conv_b_d, L3_conv_w_u, L3_conv_b_u, L3_conv_w_r, L3_conv_b_r, L3_conv_w_l, L3_conv_b_l):
    import jax
    import jax.numpy as jnp

    def _L0_conv_ref(x, experts, bias, w1, b1, w2, b2):
        import jax, jax.numpy as jnp
        import numpy as np
        STRIDE = 1
        PADDING = 1
        g = jnp.mean(x, axis=(2, 3))
        h = jax.nn.relu(g @ w1.T + b1)
        alpha = jax.nn.softmax(h @ w2.T + b2, axis=-1)
        weff = jnp.einsum('bk,koihw->boihw', alpha, experts)
        beff = jnp.einsum('bk,ko->bo', alpha, bias)
        pad = [(PADDING, PADDING), (PADDING, PADDING)]

        def conv_one(xi, wi):
            return jax.lax.conv_general_dilated(xi[None], wi, window_strides=(STRIDE, STRIDE), padding=pad, dimension_numbers=('NCHW', 'OIHW', 'NCHW'))[0]
        out = jax.vmap(conv_one)(x, weff)
        return out + beff[:, :, None, None]

    def _L1_conv_ref(x, w_d, b_d, w_u, b_u, w_r, b_r, w_l, b_l):
        import jax, jax.numpy as jnp
        import numpy as np
        import math
        C = 64
        KSIZE = 9
        PAD = KSIZE // 2

        def _conv1d(v, w, b):
            y = jax.lax.conv_general_dilated(v, w, window_strides=(1,), padding=[(PAD, PAD)], dimension_numbers=('NCH', 'OIH', 'NCH'))
            return y + b[None, :, None]

        def _sweep(x, w, b, axis, reverse):
            rows = jnp.moveaxis(x, axis, 0)
            if reverse:
                rows = rows[::-1]

            def step(prev, row):
                new = row + jax.nn.relu(_conv1d(prev, w, b))
                return (new, new)
            _, rest = jax.lax.scan(step, rows[0], rows[1:])
            out = jnp.concatenate([rows[:1], rest], axis=0)
            if reverse:
                out = out[::-1]
            return jnp.moveaxis(out, 0, axis)
        out = _sweep(x, w_d, b_d, axis=2, reverse=False)
        out = _sweep(out, w_u, b_u, axis=2, reverse=True)
        out = _sweep(out, w_r, b_r, axis=3, reverse=False)
        out = _sweep(out, w_l, b_l, axis=3, reverse=True)
        return out

    def _L2_conv_ref(x, qk_w, qk_b, lepe_w, lepe_b, num_heads):
        import jax, jax.numpy as jnp
        import numpy as np
        from jax import lax
        BASE = 10000.0

        def _rope(x):
            b, h, w, c = x.shape
            k_max = c // 2
            theta = 1.0 / BASE ** (jnp.arange(k_max, dtype=x.dtype) / k_max)
            angles = jnp.arange(h, dtype=x.dtype)[:, None] * theta
            cos = jnp.cos(angles)[None, None]
            sin = jnp.sin(angles)[None, None]
            xr = x.reshape(b, h, w, k_max, 2)
            re, im = (xr[..., 0], xr[..., 1])
            out = jnp.stack([re * cos - im * sin, re * sin + im * cos], axis=-1)
            return out.reshape(b, h, w, c)
        b, c, H, W = x.shape
        n = H * W
        hd = c // num_heads
        xf = x.reshape(b, n, c)
        qk = (xf @ qk_w.T + qk_b).reshape(b, n, 2, c)
        q = jax.nn.elu(qk[:, :, 0]) + 1.0
        k = jax.nn.elu(qk[:, :, 1]) + 1.0
        v = xf
        q_rope = _rope(q.reshape(b, H, W, c)).reshape(b, n, num_heads, hd).transpose(0, 2, 1, 3)
        k_rope = _rope(k.reshape(b, H, W, c)).reshape(b, n, num_heads, hd).transpose(0, 2, 1, 3)
        qh = q.reshape(b, n, num_heads, hd).transpose(0, 2, 1, 3)
        kh = k.reshape(b, n, num_heads, hd).transpose(0, 2, 1, 3)
        vh = v.reshape(b, n, num_heads, hd).transpose(0, 2, 1, 3)
        z = 1.0 / (jnp.einsum('bhnd,bhd->bhn', qh, kh.mean(axis=2)) + 1e-06)
        scale = float(n) ** (-0.5)
        kv = jnp.einsum('bhnd,bhne->bhde', k_rope * scale, vh * scale)
        out = jnp.einsum('bhnd,bhde->bhne', q_rope, kv) * z[..., None]
        out = out.transpose(0, 2, 1, 3).reshape(b, n, c)
        vimg = vh.transpose(0, 2, 1, 3).reshape(b, H, W, c).transpose(0, 3, 1, 2)
        lepe = lax.conv_general_dilated(vimg, lepe_w, (1, 1), 'SAME', feature_group_count=c)
        lepe = lepe + lepe_b[None, :, None, None]
        out = out + lepe.transpose(0, 2, 3, 1).reshape(b, n, c)
        return out.transpose(0, 2, 1).reshape(b, c, H, W)

    def _L3_conv_ref(x, w_d, b_d, w_u, b_u, w_r, b_r, w_l, b_l):
        import jax, jax.numpy as jnp
        import numpy as np
        import math
        C = 64
        KSIZE = 9
        PAD = KSIZE // 2

        def _conv1d(v, w, b):
            y = jax.lax.conv_general_dilated(v, w, window_strides=(1,), padding=[(PAD, PAD)], dimension_numbers=('NCH', 'OIH', 'NCH'))
            return y + b[None, :, None]

        def _sweep(x, w, b, axis, reverse):
            rows = jnp.moveaxis(x, axis, 0)
            if reverse:
                rows = rows[::-1]

            def step(prev, row):
                new = row + jax.nn.relu(_conv1d(prev, w, b))
                return (new, new)
            _, rest = jax.lax.scan(step, rows[0], rows[1:])
            out = jnp.concatenate([rows[:1], rest], axis=0)
            if reverse:
                out = out[::-1]
            return jnp.moveaxis(out, 0, axis)
        out = _sweep(x, w_d, b_d, axis=2, reverse=False)
        out = _sweep(out, w_u, b_u, axis=2, reverse=True)
        out = _sweep(out, w_r, b_r, axis=3, reverse=False)
        out = _sweep(out, w_l, b_l, axis=3, reverse=True)
        return out

    def _gn(v, G=32, eps=1e-05):
        B_, C_, H_, W_ = v.shape
        g = v.reshape(B_, G, C_ // G, H_, W_)
        m = jnp.mean(g, axis=(2, 3, 4), keepdims=True)
        s = jnp.var(g, axis=(2, 3, 4), keepdims=True)
        return ((g - m) / jnp.sqrt(s + eps)).reshape(v.shape)

    def _ln_c(v, eps=1e-06):
        m = jnp.mean(v, axis=1, keepdims=True)
        s = jnp.var(v, axis=1, keepdims=True)
        return (v - m) / jnp.sqrt(s + eps)

    def _ln_t(v, eps=1e-05):
        m = jnp.mean(v, axis=-1, keepdims=True)
        s = jnp.var(v, axis=-1, keepdims=True)
        return (v - m) / jnp.sqrt(s + eps)

    def _to_tokens(v):
        B_, C_, H_, W_ = v.shape
        return v.reshape(B_, C_, H_ * W_).transpose(0, 2, 1)

    def _from_tokens(t, like):
        B_, C_, H_, W_ = like.shape
        return t.transpose(0, 2, 1).reshape(B_, C_, H_, W_)
    x = x + _L0_conv_ref(_gn(x), L0_conv_experts, L0_conv_bias, L0_conv_w1, L0_conv_b1, L0_conv_w2, L0_conv_b2)
    x = x + _L1_conv_ref(_gn(x), L1_conv_w_d, L1_conv_b_d, L1_conv_w_u, L1_conv_b_u, L1_conv_w_r, L1_conv_b_r, L1_conv_w_l, L1_conv_b_l)
    x = x + _L2_conv_ref(_gn(x), L2_conv_qk_w, L2_conv_qk_b, L2_conv_lepe_w, L2_conv_lepe_b, 8)
    x = x + _L3_conv_ref(_gn(x), L3_conv_w_d, L3_conv_b_d, L3_conv_w_u, L3_conv_b_u, L3_conv_w_r, L3_conv_b_r, L3_conv_w_l, L3_conv_b_l)
    return x

_drawn_inputs = setup_inputs


def setup_inputs(seed=0):
    import zlib

    import numpy as np

    out = dict(_drawn_inputs(seed))
    spreads = {'L0_conv_bias': (0.0, 0.1),
     'L0_conv_b1': (0.0, 0.8),
     'L0_conv_b2': (0.0, 0.474),
     'L2_conv_qk_b': (0.0, 2.0),
     'L2_conv_lepe_b': (0.0, 0.1)}
    factors = {'L0_conv_w1': 64.0,
     'L0_conv_w2': 8.0,
     'L1_conv_b_d': 8.0,
     'L1_conv_b_u': 8.0,
     'L1_conv_b_r': 8.0,
     'L1_conv_b_l': 8.0,
     'L2_conv_qk_w': 36.511,
     'L3_conv_b_d': 27.844,
     'L3_conv_b_u': 29.037,
     'L3_conv_b_r': 23.955,
     'L3_conv_b_l': 27.096}
    for name, (base, spread) in spreads.items():
        noise = np.random.default_rng([zlib.crc32(name.encode()), seed]).standard_normal(out[name].shape)
        drawn = base * np.exp(spread * noise) if base else spread * noise
        out[name] = jnp.asarray(drawn.astype(out[name].dtype))
    for name, factor in factors.items():
        out[name] = (out[name] * factor).astype(out[name].dtype)
    return out
```

```python
from contextlib import ExitStack

import concourse.bass as bass
from concourse import mybir

P = 128
B, C, H, W = 16, 64, 64, 64
HALF = 64
J = 32
GROUPS = 32
KTAPS = 9
NBLK = 5
NB = B // 2
PADJ = 2
STEPS = 63

F32 = mybir.dt.float32
F32R = mybir.dt.float32r
I32 = mybir.dt.int32
ALU = mybir.AluOpType
ACT = mybir.ActivationFunctionType
AX_X = mybir.AxisListType.X


def semaphores(nc, ctx, tag):
    taken = []

    def sem(name):
        taken.append(nc.alloc_semaphore(name=f"{tag}_{name}"))
        return taken[-1]

    def clear():
        nc.clear_and_free_semaphores(taken)
        nc.all_engine_barrier()

    ctx.callback(clear)
    return sem


def sweep_pair(nc, ctx, S, base, w_taps, biases, tag):
    def sb(name, shape, dt=F32):
        return ctx.enter_context(nc.sbuf_tensor(f"{tag}_{name}", shape, dt))

    sem = semaphores(nc, ctx, tag)

    w_raw = sb("w_raw", [P, 2, NBLK * P])
    w_hi = sb("w_hi", [P, 2, NBLK * P], F32R)
    w_lo = sb("w_lo", [P, 2, NBLK * P], F32R)
    bias = sb("bias", [P, 2])
    neg_bias = sb("neg_bias", [P, 2])
    row_b = [sb(f"row_b{p}", [P, NB, J]) for p in range(2)]
    x_hi = [sb(f"x_hi{p}", [P, NB, J + 2 * PADJ], F32R) for p in range(2)]
    x_lo = [sb(f"x_lo{p}", [P, NB, J + 2 * PADJ], F32R) for p in range(2)]
    conv = [ctx.enter_context(nc.psum_tensor(f"{tag}_conv{p}", [P, 512], F32)) for p in range(2)]

    w_zeroed = sem("w_zeroed")
    w_loaded = sem("w_loaded")
    b_loaded = sem("b_loaded")
    b_ready = sem("b_ready")
    w_hi_ready = sem("w_hi_ready")
    w_ready = sem("w_ready")
    pads_ready = sem("pads_ready")
    row_b_ready = [sem(f"row_b_ready{p}") for p in range(2)]
    conv_done = [sem(f"conv_done{p}") for p in range(2)]
    new_ready = [sem(f"new_ready{p}") for p in range(2)]
    hi_ready = [sem(f"hi_ready{p}") for p in range(2)]
    lo_ready = [sem(f"lo_ready{p}") for p in range(2)]

    def slots(p):
        return slice(base + p * NB, base + (p + 1) * NB)

    with nc.Block() as block:

        @block.sync
        def _(sp):
            sp.wait_ge(w_zeroed, 1)
            for k in range(2):
                blocks = w_raw[:, k, :].rearrange("p (s o c) -> p s o c", s=NBLK, o=2)
                for pi in range(2):
                    for po in range(2):
                        s0 = 1 if pi < po else 0
                        s1 = NBLK - 1 if pi > po else NBLK
                        t0 = 2 * s0 + pi - po
                        sp.dma_start(blocks[pi * HALF:(pi + 1) * HALF, s0:s1, po, :],
                                     w_taps[k][:, t0:t0 + 2 * (s1 - s0) - 1:2, :]).then_inc(w_loaded, 16)

        @block.gpsimd
        def _(pool):
            for k in range(2):
                for half in range(2):
                    pool.dma_start(bias[half * HALF:(half + 1) * HALF, k:k + 1],
                                   biases[k].rearrange("(c a) -> c a", a=1)).then_inc(b_loaded, 16)

        @block.scalar
        def _(act):
            act.wait_ge(b_loaded, 64)
            for k in range(2):
                with act.Fori(0, STEPS) as i:
                    row = act.snap(i + 1 if k == 0 else i * -1 + (STEPS - 1))
                    step = act.snap(i + (k * STEPS + 1))
                    for p in range(2):
                        act.wait_ge(hi_ready[p], step)
                        nc.scalar.activation(row_b[p][:, :, :], S[:, slots(p), bass.ds(row, 1), :],
                                             ACT.Identity, bias=bias[:, k:k + 1]).then_inc(row_b_ready[p], 1)

        @block.vector
        def _(dve):
            nc.vector.memset(w_raw[:, :, :], 0.0).then_inc(w_zeroed, 1)
            for p in range(2):
                nc.vector.memset(x_hi[p][:, :, :].bitcast(F32), 0.0).then_inc(pads_ready, 1)
                nc.vector.memset(x_lo[p][:, :, :].bitcast(F32), 0.0).then_inc(pads_ready, 1)
            dve.wait_ge(b_loaded, 64)
            nc.vector.tensor_scalar_mul(neg_bias[:, :], bias[:, :], -1.0).then_inc(b_ready, 1)
            dve.wait_ge(pads_ready, 4)
            for p in range(2):
                nc.vector.tensor_copy(x_hi[p][:, :, PADJ:PADJ + J], S[:, slots(p), 0, :]).then_inc(hi_ready[p], 1)
                dve.wait_ge(hi_ready[p], 1)
                nc.vector.tensor_tensor(x_lo[p][:, :, PADJ:PADJ + J], S[:, slots(p), 0, :],
                                        x_hi[p][:, :, PADJ:PADJ + J].bitcast(F32), ALU.subtract).then_inc(lo_ready[p], 1)
            dve.wait_ge(w_loaded, 8 * 16)
            nc.vector.tensor_copy(w_hi[:, :, :], w_raw[:, :, :]).then_inc(w_hi_ready, 1)
            dve.wait_ge(w_hi_ready, 1)
            nc.vector.tensor_tensor(w_lo[:, :, :], w_raw[:, :, :], w_hi[:, :, :].bitcast(F32),
                                    ALU.subtract).then_inc(w_ready, 1)
            dve.wait_ge(b_ready, 1)
            for k in range(2):
                with dve.Fori(0, STEPS) as i:
                    row = dve.snap(i + 1 if k == 0 else i * -1 + (STEPS - 1))
                    step = dve.snap(i + (k * STEPS + 1))
                    for p in range(2):
                        new = S[:, slots(p), bass.ds(row, 1), :]
                        dve.wait_ge(row_b_ready[p], step)
                        dve.wait_ge(conv_done[p], step)
                        nc.vector.scalar_tensor_tensor(
                            out=new, in0=conv[p][:, 0:NB * J].rearrange("p (b j) -> p b j", b=NB),
                            scalar=neg_bias[:, k:k + 1], in1=row_b[p][:, :, :],
                            op0=ALU.max, op1=ALU.add).then_inc(new_ready[p], 1)
                        dve.wait_ge(new_ready[p], step)
                        nc.vector.tensor_scalar(x_hi[p][:, :, PADJ:PADJ + J], new, 1.0, None, ALU.mult).then_inc(hi_ready[p], 1)
                        dve.wait_ge(hi_ready[p], step + 1)
                        nc.vector.tensor_tensor(x_lo[p][:, :, PADJ:PADJ + J], new,
                                                x_hi[p][:, :, PADJ:PADJ + J].bitcast(F32),
                                                ALU.subtract).then_inc(lo_ready[p], 1)

        @block.tensor
        def _(pe):
            pe.wait_ge(w_ready, 1)
            for k in range(2):
                with pe.Fori(0, STEPS) as i:
                    step = pe.snap(i + (k * STEPS + 1))
                    for p in range(2):
                        out = conv[p][:, 0:NB * J]
                        pe.wait_ge(hi_ready[p], step)
                        for s in range(NBLK):
                            for n, w in enumerate((w_hi, w_lo)):
                                nc.tensor.matmul(out, w[:, k, s * P:(s + 1) * P], x_hi[p][:, :, s:s + J],
                                                 start=(s == 0 and n == 0), stop=False)
                        pe.wait_ge(lo_ready[p], step)
                        for s in range(NBLK):
                            mm = nc.tensor.matmul(out, w_hi[:, k, s * P:(s + 1) * P], x_lo[p][:, :, s:s + J],
                                                  start=False, stop=(s == NBLK - 1))
                        mm.then_inc(conv_done[p], 1)


def relayout(nc, ctx, S, tag):
    sem = semaphores(nc, ctx, tag)
    moved = [sem(f"moved_{e}") for e in ("dve", "act")]

    def quarter(b, pw, ph):
        src = S[pw * HALF:(pw + 1) * HALF, bass.ds(b + 1, 1), :, :].rearrange("p a (h q) w -> p (a q) h w", q=2)[:, ph]
        dst = S[ph * HALF:(ph + 1) * HALF, bass.ds(b, 1), :, :].rearrange("p a (w q) h -> p (a q) h w", q=2)[:, pw]
        return dst, src

    with nc.Block() as block:
        @block.vector
        def _(dve):
            with dve.Fori(0, B) as b:
                for pw in range(2):
                    nc.vector.tensor_copy(*quarter(b, pw, 0)).then_inc(moved[0], 1)
                done = dve.snap(b * 2 + 2)
                dve.wait_ge(moved[0], done)
                dve.wait_ge(moved[1], done)

        @block.scalar
        def _(act):
            with act.Fori(0, B) as b:
                for pw in range(2):
                    nc.scalar.copy(*quarter(b, pw, 1)).then_inc(moved[1], 1)
                done = act.snap(b * 2 + 2)
                act.wait_ge(moved[0], done)
                act.wait_ge(moved[1], done)


def wait_from(eng, sem, value):
    if not isinstance(value, int) or value > 0:
        eng.wait_ge(sem, value)


CH = 4
CB = J // CH
WP = W + 2
KE = 4
HID = 32
PER_LOOP = 29
XN = [4, 7, 10, 14]
PER = 4
TURNS = 3
GN_EPS = 1e-5


class Chain:

    def __init__(self, eng, sem):
        self.eng, self.sem, self.count, self.offset = eng, sem, 0, 0

    def step(self, instruction):
        instruction.then_inc(self.sem, 1)
        self.count += 1
        self.eng.wait_ge(self.sem, self.offset + self.count)

    def carry(self, pause):
        self.eng.tensor_tensor(pause, pause, pause, ALU.mult).then_inc(self.sem, 1)
        self.count += 1

    def turn(self, t, per_turn):
        self.offset, self.per_turn, self.start = t * per_turn, per_turn, self.count

    def leave(self, turns):
        assert self.count - self.start == self.per_turn, self.count - self.start
        self.count += (turns - 1) * self.per_turn
        self.offset = 0


NEWTON_STEPS = 11


def newton_rsqrt(eng, chain, out, guess, half_var, one_half, tmp, ready):
    for i in range(3):
        chain.step(eng.tensor_tensor(tmp, guess, guess, ALU.mult))
        chain.step(eng.tensor_tensor(tmp, tmp, half_var, ALU.mult))
        chain.step(eng.tensor_tensor(tmp, one_half, tmp, ALU.subtract))
        if i < 2:
            chain.step(eng.tensor_tensor(guess, guess, tmp, ALU.mult))
    eng.tensor_tensor(out, guess, tmp, ALU.mult).then_inc(ready, 1)


def rsqrt_guess(nc, chain, guess, half, var):
    chain.step(nc.vector.tensor_scalar(half.bitcast(I32), var.bitcast(I32), 1, None, ALU.logical_shift_right))
    chain.step(nc.vector.tensor_scalar(var, var, 0.5, None, ALU.mult))
    return nc.vector.tensor_scalar(guess.bitcast(I32), half.bitcast(I32), -1.0, float(0x5f3759df), ALU.mult, ALU.add)


def dyn_conv(nc, ctx, S, x_in, x1_out, experts, bias_k, w1, b1, w2, b2, group_avg):
    def sb(name, shape, dt=F32):
        return ctx.enter_context(nc.sbuf_tensor(f"dc_{name}", shape, dt))

    sem = semaphores(nc, ctx, "dc")

    raw = [sb(f"raw{u}", [P, J, W]) for u in range(PER)]
    xn = S[:, 0, :, :].rearrange("p a b -> p (a b)").rearrange("p (u m i w) -> p u m i w", u=2, m=2, i=CB)
    xz_hi = [sb(f"xz_hi{u}", [P, 2, CB, WP], F32R) for u in range(2)]
    xz_lo = [sb(f"xz_lo{u}", [P, 2, CB, WP], F32R) for u in range(2)]
    ex = sb("ex", [P, KE, 2 * 3, P])
    w_mix = sb("w_mix", [P, 2 * 3, P])
    w_hi = sb("w_hi", [P, 2 * 3, P], F32R)
    w_lo = sb("w_lo", [P, 2 * 3, P], F32R)
    avg = sb("avg", [P, P])
    ones = sb("ones", [HID, P])
    w1s = sb("w1s", [P, HID])
    zeros = sb("zeros", [P, W])
    bn = sb("bn", [P, 2, CH, 6])
    small = sb("small", [P, 72])
    pause = small[:, 70:71]
    b1s, h, w2s, w2h = small[0:HID, 0:1], small[0:HID, 1:2], small[0:HID, 4:8], small[0:HID, 8:12]
    b2s, bks = small[:, 12:16], small[:, 16:20]
    logit, prob, alpha, bprod = small[:, 20:24], small[:, 24:28], small[:, 28:32], small[:, 32:36]
    top, total, beff, gmean = small[:, 36:37], small[:, 37:38], small[:, 38:39], small[:, 39:40]
    stat = [small[:, 40 + 4 * i:44 + 4 * i].rearrange("p (a b) -> p a b", a=2) for i in range(3)]
    mv, me, gs = stat
    sq = small[:, 52:54]
    var = small[:, 54:56]
    guess, sq_pool, three_halves = small[:, 64:66], small[:, 66:68], small[:, 68:70]
    affine = [small[:, 56 + 4 * u:60 + 4 * u].rearrange("p (b a) -> p b a", b=2) for u in range(2)]

    conv = [ctx.enter_context(nc.psum_tensor(f"dc_conv{u}", [P, 512], F32)) for u in range(2)]
    tiny = ctx.enter_context(nc.psum_tensor("dc_tiny", [P, 512], F32))
    hid_ps, logit_ps = tiny[0:HID, 8:9], tiny[:, 16:16 + KE]
    group_ps = tiny[:, 0:4].rearrange("p (a b) -> p a b", a=2)

    consts_in, ex_zeroed, ex_in, set_up = sem("consts_in"), sem("ex_zeroed"), sem("ex_in"), sem("set_up")
    raw_in = [sem(f"raw_in{u}") for u in range(PER)]
    x1_stored, s_done = sem("x1_stored"), sem("s_done")
    xn_ready, hi_ready, lox_ready, loz_ready = sem("xn_ready"), sem("hi_ready"), sem("lox_ready"), sem("loz_ready")
    conv_done, evac_done, w_ready = sem("conv_done"), sem("evac_done"), sem("w_ready")
    me_ready, group_done, var_ready = sem("me_ready"), sem("group_done"), sem("var_ready")
    rstd_ready, affine_ready, gmean_ready = sem("rstd_ready"), sem("affine_ready"), sem("gmean_ready")
    hid_done, h_ready, w2h_ready = sem("hid_done"), sem("h_ready"), sem("w2h_ready")
    logit_done, logit_ready, prob_ready = sem("logit_done"), sem("logit_ready"), sem("prob_ready")
    dve_step, pool_step = sem("dve_step"), sem("pool_step")
    RES, INP, BOTH = slice(0, 1), slice(1, 2), slice(0, 2)

    def chunk(t, q):
        return t[:, q * CB:(q + 1) * CB, :].rearrange("p i w -> p (i w)")

    def cols(n):
        return INP if isinstance(n, int) and n == 0 else RES if isinstance(n, int) and n == B - 1 else BOTH

    def walk(eng, sample, chain=None, per_turn=0):
        sample(0, 0)
        sample(0, 1)
        with eng.Fori(0, TURNS) as t:
            if chain:
                chain.turn(t, per_turn)
            for k in range(2, 2 + PER):
                sample(t, k)
        if chain:
            chain.leave(TURNS)
        sample(TURNS, 2)
        sample(TURNS, 3)

    with nc.Block() as block:

        @block.sync
        def _(sp):
            def load(n, u):
                for half in range(2):
                    sp.dma_start(raw[u][half * HALF:(half + 1) * HALF, :, :],
                                 x_in[bass.ds(n, 1), :, :, half, :].rearrange("a c i w -> (a c) i w")
                                 ).then_inc(raw_in[u], 16)

            def store(n, u):
                sp.wait_ge(evac_done, n * CH + CH)
                sp.dma_start(x1_out[bass.ds(n, 1), :, :].rearrange("a p f -> (a p) f"),
                             raw[u][:, :, :].rearrange("p i w -> p (i w)")).then_inc(x1_stored, 16)

            for n in range(PER):
                load(n, n)
            with sp.Fori(0, B // PER - 1) as t:
                for u in range(PER):
                    n = t * PER + u
                    store(n, u)
                    sp.wait_ge(x1_stored, n * 16 + 16)
                    sp.wait_ge(s_done, n * 4 + 4)
                    load(n + PER, u)
            for n in range(B - PER, B):
                store(n, n % PER)
            sp.wait_ge(x1_stored, 16 * B)

        @block.gpsimd
        def _(pool):
            pool.dma_start(avg[:, :], group_avg).then_inc(consts_in, 16)
            for half in range(2):
                pool.dma_start(w1s[half * HALF:(half + 1) * HALF, :], w1).then_inc(consts_in, 16)
                pool.dma_start(bks[half * HALF:(half + 1) * HALF, :], bias_k).then_inc(consts_in, 16)
            pool.dma_start(b1s, b1.rearrange("(c a) -> c a", a=1)).then_inc(consts_in, 16)
            pool.dma_start(w2s, w2).then_inc(consts_in, 16)
            pool.dma_start(b2s, b2.rearrange("(a k) -> a k", a=1).to_broadcast([P, KE])).then_inc(consts_in, 16)
            pool.wait_ge(ex_zeroed, 1)
            for m, pi, po, kh in ((0, 0, 0, 1), (0, 0, 1, 0), (0, 1, 0, 2), (0, 1, 1, 1), (1, 0, 1, 2), (1, 1, 0, 0)):
                for k in range(KE):
                    pool.dma_start(ex[pi * HALF:(pi + 1) * HALF, k, 3 * m:3 * m + 3, po * C:(po + 1) * C],
                                   experts[:, k, kh, :, :]).then_inc(ex_in, 16)

            chain = Chain(pool, pool_step)

            def rstd(r, parity, c):
                pool.wait_ge(var_ready, r + 1)
                newton_rsqrt(nc.gpsimd, chain, affine[parity][:, 0, c], guess[:, c], var[:, c], three_halves[:, c], sq_pool[:, c], rstd_ready)

            def sample(t, k):
                n = t * PER + k
                for q in range(CH):
                    g, u = n * CH + q, q % 2
                    pool.wait_ge(hi_ready, g + 1)
                    nc.gpsimd.tensor_tensor(xz_lo[u][:, 1, :, 1:W + 1], xn[:, u, 1, :, :],
                                            xz_hi[u][:, 1, :, 1:W + 1].bitcast(F32),
                                            ALU.subtract).then_inc(loz_ready, 1)
                    if q == 1:
                        rstd(n + 1, k % 2, cols(n))

            pool.wait_ge(set_up, 7)
            rstd(0, 1, INP)
            walk(pool, sample, chain, PER * NEWTON_STEPS)
            rstd(B + 1, 0, RES)

        @block.scalar
        def _(act):
            def normalise(t, k, q):
                n, u, x = t * PER + k, q % 2, raw[k % PER]
                scale, shift = affine[(k + 1) % 2][:, 0, INP], affine[(k + 1) % 2][:, 1, INP]
                ev, od = slice(0, HALF), slice(HALF, P)
                act.wait_ge(affine_ready, n + 1)
                wait_from(act, lox_ready, n * CH + (q - 1))
                wait_from(act, loz_ready, n * CH + (q - 1))
                parts = [(slice(0, P), 0, 0, q * CB, CB), (ev, 1, 0, q * CB + 1, CB), (od, 1, 0, q * CB - 1, CB)]
                if q == 0:
                    parts[2] = (od, 1, 1, 0, CB - 1)
                    nc.scalar.activation(xn[od, u, 1, 0, :], zeros[od, :], ACT.Identity).then_inc(xn_ready, 1)
                if q == CH - 1:
                    parts[1] = (ev, 1, 0, q * CB + 1, CB - 1)
                    nc.scalar.activation(xn[ev, u, 1, CB - 1, :], zeros[ev, :], ACT.Identity).then_inc(xn_ready, 1)
                for part, m, to, at, rows in parts:
                    nc.scalar.activation(xn[part, u, m, to:to + rows, :], x[part, at:at + rows, :], ACT.Identity,
                                         bias=shift[part, :], scale=scale[part, :]).then_inc(xn_ready, 1)

            def hidden(m):
                act.wait_ge(hid_done, m + 1)
                nc.scalar.activation(h, hid_ps, ACT.Relu, bias=b1s, scale=0.5).then_inc(h_ready, 1)

            def exps(m):
                act.wait_ge(logit_ready, m + 1)
                nc.scalar.activation(prob, logit, ACT.Exp, accum_out=total).then_inc(prob_ready, 1)

            def sample(t, k):
                n = t * PER + k
                last = isinstance(n, int) and n == B - 1
                for q in range(1, CH):
                    normalise(t, k, q)
                if not last:
                    hidden(n + 1)
                    normalise(t, k + 1, 0)
                    exps(n + 1)

            act.wait_ge(set_up, 7)
            act.wait_ge(consts_in, 8 * 16)
            hidden(0)
            normalise(0, 0, 0)
            exps(0)
            walk(act, sample)

        @block.tensor
        def _(pe):
            def group(r, c):
                pe.wait_ge(me_ready, r + 1)
                nc.tensor.matmul(group_ps[:, c, :], avg[:, :], me[:, c, :], start=True, stop=True).then_inc(group_done, 1)

            def hid(m):
                pe.wait_ge(gmean_ready, m + 1)
                nc.tensor.matmul(hid_ps, w1s[:, :], gmean, start=True, stop=True).then_inc(hid_done, 1)

            def logits(m):
                pe.wait_ge(w2h_ready, m + 1)
                nc.tensor.matmul(logit_ps, ones[:, :], w2h, start=True, stop=True).then_inc(logit_done, 1)

            def sample(t, k):
                n = t * PER + k
                last = isinstance(n, int) and n == B - 1
                for q in range(CH):
                    g, u = n * CH + q, q % 2
                    pe.wait_ge(hi_ready, g + 1)
                    wait_from(pe, evac_done, g - 1)
                    if q == 0:
                        pe.wait_ge(w_ready, n + 1)
                    for m in range(2):
                        for dw in range(3):
                            for j, w in enumerate((w_hi, w_lo)):
                                nc.tensor.matmul(conv[u][:, :], w[:, 3 * m + dw, :], xz_hi[u][:, m, :, dw:dw + W],
                                                 start=(m == dw == j == 0), stop=False)
                        if m == 0 and q == 1:
                            group(n + 1, cols(n))
                        if m == 0 and q == 2 and not last:
                            hid(n + 1)
                        if m == 0 and q == 3 and not last:
                            logits(n + 1)
                    pe.wait_ge(lox_ready, g + 1)
                    pe.wait_ge(loz_ready, g + 1)
                    for m in range(2):
                        for dw in range(3):
                            mm = nc.tensor.matmul(conv[u][:, :], w_hi[:, 3 * m + dw, :], xz_lo[u][:, m, :, dw:dw + W],
                                                  start=False, stop=(m == 1 and dw == 2))
                    mm.then_inc(conv_done, 1)

            pe.wait_ge(consts_in, 8 * 16)
            pe.wait_ge(set_up, 7)
            group(0, INP)
            hid(0)
            logits(0)
            walk(pe, sample)
            group(B + 1, RES)

        @block.vector
        def _(dve):
            chain = Chain(dve, dve_step)

            def input_stats(t, k):
                dve.wait_ge(raw_in[k % PER], t * 32 + 32 * (k // PER + 1))
                for q in range(CH):
                    nc.vector.bn_stats(bn[:, 1, q, :], chunk(raw[k % PER], q)).then_inc(dve_step, 1)
                    chain.count += 1
                dve.wait_ge(dve_step, chain.offset + chain.count)
                chain.carry(pause)
                chain.step(nc.vector.bn_aggr(mv[:, 1, :], bn[:, 1, :, :]))

            def result_stats():
                chain.carry(pause)
                chain.step(nc.vector.bn_aggr(mv[:, 0, :], bn[:, 0, :, :]))

            def squares(c):
                chain.step(nc.vector.tensor_tensor(sq[:, c], mv[:, c, 0], mv[:, c, 0], ALU.mult))
                nc.vector.tensor_copy(me[:, c, 0], mv[:, c, 0])
                nc.vector.tensor_tensor(me[:, c, 1], sq[:, c], mv[:, c, 1], ALU.add).then_inc(me_ready, 1)

            def group_affine(r, parity, c):
                dve.wait_ge(group_done, r + 1)
                chain.step(nc.vector.tensor_copy(gs[:, c, :], group_ps[:, c, :]))
                chain.step(nc.vector.tensor_tensor(sq[:, c], gs[:, c, 0], gs[:, c, 0], ALU.mult))
                chain.step(nc.vector.scalar_tensor_tensor(out=var[:, c], in0=gs[:, c, 1], scalar=GN_EPS, in1=sq[:, c],
                                                          op0=ALU.add, op1=ALU.subtract))
                rsqrt_guess(nc, chain, guess[:, c], sq[:, c], var[:, c]).then_inc(var_ready, 1)
                dve.wait_ge(rstd_ready, r + 1)
                nc.vector.scalar_tensor_tensor(out=affine[parity][:, 1, c], in0=gs[:, c, 0], scalar=-1.0,
                                               in1=affine[parity][:, 0, c], op0=ALU.mult,
                                               op1=ALU.mult).then_inc(affine_ready, 1)
                dve.wait_ge(affine_ready, r + 1)

            def gate_mean(parity):
                nc.vector.tensor_scalar(gmean, mv[:, INP, 0], affine[parity][:, 0, INP], affine[parity][:, 1, INP],
                                        ALU.mult, ALU.add).then_inc(gmean_ready, 1)

            def to_slot(n, u, parity):
                for ph in range(2):
                    part = slice(ph * HALF, (ph + 1) * HALF)
                    for pw in range(2):
                        dst = S[pw * HALF:(pw + 1) * HALF, bass.ds(n + 1, 1), :, :].rearrange(
                            "p a (h q) w -> p (a q) h w", q=2)[:, ph]
                        src = raw[u][part, :, :].rearrange("p i (w q) -> p q i w", q=2)[:, pw]
                        nc.vector.tensor_scalar(dst, src, affine[parity][part, 0, RES], affine[parity][part, 1, RES],
                                                ALU.mult, ALU.add).then_inc(s_done, 1)

            def gate_hidden(m):
                dve.wait_ge(h_ready, m + 1)
                nc.vector.tensor_scalar(w2h, w2s, h, None, ALU.mult).then_inc(w2h_ready, 1)

            def mix(m):
                dve.wait_ge(logit_done, m + 1)
                chain.step(nc.vector.tensor_tensor(logit, logit_ps, b2s, ALU.add))
                chain.step(nc.vector.reduce_max(top, logit, AX_X))
                nc.vector.tensor_scalar(logit, logit, top, None, ALU.subtract).then_inc(logit_ready, 1)
                dve.wait_ge(prob_ready, m + 1)
                chain.step(nc.vector.reciprocal(total, total))
                chain.step(nc.vector.tensor_scalar(alpha, prob, total, None, ALU.mult))
                chain.step(nc.vector.tensor_scalar(w_mix[:, :, :], ex[:, 0, :, :], alpha[:, 0:1], None, ALU.mult))
                for k in range(1, KE):
                    chain.step(nc.vector.scalar_tensor_tensor(out=w_mix[:, :, :], in0=ex[:, k, :, :],
                                                              scalar=alpha[:, k:k + 1], in1=w_mix[:, :, :],
                                                              op0=ALU.mult, op1=ALU.add))

            def split_weights():
                chain.step(nc.vector.tensor_copy(w_hi[:, :, :], w_mix[:, :, :]))
                nc.vector.tensor_tensor(w_lo[:, :, :], w_mix[:, :, :], w_hi[:, :, :].bitcast(F32),
                                        ALU.subtract).then_inc(w_ready, 1)

            def split_chunk(n, q):
                g, u = n * CH + q, q % 2
                dve.wait_ge(xn_ready, n * XN[-1] + XN[q])
                wait_from(dve, conv_done, g - 1)
                nc.vector.tensor_copy(xz_hi[u][:, :, :, 1:W + 1], xn[:, u, :, :, :]).then_inc(hi_ready, 1)
                dve.wait_ge(hi_ready, g + 1)
                nc.vector.tensor_tensor(xz_lo[u][:, 0, :, 1:W + 1], xn[:, u, 0, :, :],
                                        xz_hi[u][:, 0, :, 1:W + 1].bitcast(F32), ALU.subtract).then_inc(lox_ready, 1)

            def residual(g, u_raw, q):
                dve.wait_ge(conv_done, g + 1)
                x = chunk(raw[u_raw], q)
                nc.vector.scalar_tensor_tensor(out=x, in0=conv[q % 2][:, :], scalar=beff, in1=x,
                                               op0=ALU.add, op1=ALU.add).then_inc(evac_done, 1)
                dve.wait_ge(evac_done, g + 1)
                nc.vector.bn_stats(bn[:, 0, q, :], x).then_inc(dve_step, 1)
                chain.count += 1

            def effective_bias():
                chain.step(nc.vector.tensor_tensor(bprod, bks, alpha, ALU.mult))
                chain.step(nc.vector.reduce_sum(beff, bprod, AX_X))

            def sample(t, k):
                n = t * PER + k
                first, last = isinstance(n, int) and n == 0, isinstance(n, int) and n == B - 1
                for q in range(CH):
                    split_chunk(n, q)
                    if q == 0:
                        wait_from(dve, conv_done, n * CH)
                        split_weights()
                    if not (first and q == 0):
                        residual(n * CH + (q - 1), (k - (q == 0)) % PER, (q - 1) % CH)
                    if q == 0:
                        effective_bias()
                        if not first:
                            result_stats()
                        if not last:
                            input_stats(t, k + 1)
                        squares(cols(n))
                    if q == 1:
                        group_affine(n + 1, k % 2, cols(n))
                        if not last:
                            gate_mean(k % 2)
                        if not first:
                            to_slot(n - 1, (k - 1) % PER, k % 2)
                    if q == 2 and not last:
                        gate_hidden(n + 1)
                    if q == 3 and not last:
                        mix(n + 1)

            nc.vector.memset(ex[:, :, :, :], 0.0).then_inc(ex_zeroed, 1)
            for t in (*xz_hi, *xz_lo):
                nc.vector.memset(t[:, :, :, :].bitcast(F32), 0.0).then_inc(set_up, 1)
            nc.vector.memset(ones[:, :], 1.0).then_inc(set_up, 1)
            nc.vector.memset(zeros[:, :], 0.0)
            nc.vector.memset(three_halves, 1.5).then_inc(set_up, 1)
            nc.vector.memset(pause, 1.0).then_inc(set_up, 1)
            dve.wait_ge(set_up, 7)
            dve.wait_ge(consts_in, 8 * 16)
            input_stats(0, 0)
            squares(INP)
            group_affine(0, 1, INP)
            gate_mean(1)
            gate_hidden(0)
            dve.wait_ge(ex_in, 6 * KE * 16)
            mix(0)
            walk(dve, sample, chain, PER * PER_LOOP)
            residual(B * CH - 1, B % PER - 1, CH - 1)
            dve.wait_ge(dve_step, chain.count)
            result_stats()
            squares(RES)
            group_affine(B + 1, 0, RES)
            to_slot(B - 1, (B - 1) % PER, 0)


HEADS, HD = 8, 8
QR = 8
PE_TAPS = [(1, 1), (0, 1), (2, 1), (0, 0)]
DVE_TAPS = [(1, 0), (1, 2), (0, 2), (2, 0), (2, 2)]


def attention(nc, ctx, S, x1, x2, x3, consts, cos_k, sin_k, cos_q, sin_q, wqk, bqk, lepe_w, lepe_b):
    def sb(name, shape, dt=F32):
        return ctx.enter_context(nc.sbuf_tensor(f"at_{name}", shape, dt))

    sem = semaphores(nc, ctx, "at")

    xr = sb("xr", [P, J, W])
    G = sb("G", [P, J, W])
    T = sb("T", [P, J + 2, C])
    res = sb("res", [P, C, J])
    kt = [sb(f"kt{u}", [P, 8, W]) for u in range(2)]
    ke = sb("ke", [P, 8, W])
    kcs = sb("kcs", [P, 8, 2, W])
    lepe = [kcs[:, 4 * u:4 * u + 4, :, :].rearrange("p i s w -> p (i s) w") for u in range(2)]
    tab_k = sb("tab_k", [P, 2, J, J])
    tab_q = sb("tab_q", [P, 2, J])
    qe = [sb(f"qe{u}", [P, QR, C]) for u in range(2)]
    qr = [sb(f"qr{u}", [P, QR, C]) for u in range(2)]
    qs = sb("qs", [P, QR, C])
    zs = sb("zs", [P, QR, C])
    cst = sb("cst", [P, 6, P])
    avg, ident, mask, rot1, rot2, same_j = (cst[:, i, :] for i in range(6))
    wq = sb("wq", [P, P])
    wk = sb("wk", [P, P])
    diag = sb("diag", [P, len(PE_TAPS), P])
    ab = sb("ab", [P, W])
    kvw = sb("kvw", [P, 3, P])
    bk = sb("bk", [P, W])
    ones = sb("ones", [P, 1])
    small = sb("small", [P, 64])
    lw, lb, bq, ks = small[:, 0:9], small[:, 9:10], small[:, 10:11], small[:, 11:12]
    eps_z = small[:, 12:13]
    stat = [small[:, 16 + 4 * i:20 + 4 * i].rearrange("p (a b) -> p a b", a=2) for i in range(3)]
    mv, me, gs = stat
    sq, var, guess, sq_pool = (small[:, 28 + 2 * i:30 + 2 * i] for i in range(4))
    three_halves, pause = small[:, 40:42], small[:, 42:43]
    affine = small[:, 36:40].rearrange("p (b a) -> p b a", b=2)
    bn = sb("bn", [P, 2, 4, 6])

    bank = lambda name: ctx.enter_context(nc.psum_tensor(f"at_ps_{name}", [P, 512], F32))
    tk_ps = [bank("tk0"), bank("tk1")]
    q_ps, z_ps, out_ps, lepe_ps, ab_ps, tiny = (bank(x) for x in ("q", "z", "out", "lepe", "ab", "tiny"))
    group_ps, ksp_ps, ks_ps = tiny[:, 0:4].rearrange("p (a b) -> p a b", a=2), tiny[:, 8:9], tiny[:, 16:17]
    rot_ps = [tiny[:, 64:128], tiny[:, 128:192]]

    consts_in, set_up = sem("consts_in"), sem("set_up")
    x1_in, x2_ready, x2_stored, res_in, x3_stored = sem("x1_in"), sem("x2_ready"), sem("x2_stored"), sem("res_in"), sem("x3_stored")
    g_ready, tr_done, t_ready, k_done = sem("g_ready"), sem("tr_done"), sem("t_ready"), sem("k_done")
    kt_ready, ke_ready, kr_ready, kk_ready, kc_ready, ks_ready = (sem(x) for x in ("kt_ready", "ke_ready", "kr_ready", "kk_ready", "kc_ready", "ks_ready"))
    kv_done, ab_ready, rot_done, kvw_ready = sem("kv_done"), sem("ab_ready"), sem("rot_done"), sem("kvw_ready")
    q_done, qe_ready, qr_ready, qq_ready, qc_ready, qs_ready = (sem(x) for x in ("q_done", "qe_ready", "qr_ready", "qq_ready", "qc_ready", "qs_ready"))
    z_done, zs_ready, lepe_done, lepe_added, out_done, out_scaled = (sem(x) for x in ("z_done", "zs_ready", "lepe_done", "lepe_added", "out_done", "out_scaled"))
    taps_done, both_ready, out_added, s_done = sem("taps_done"), sem("both_ready"), sem("out_added"), sem("s_done")
    me_ready, group_done, var_ready, rstd_ready, affine_ready = ([sem(f"{x}{i}") for i in range(2)] for x in ("me_ready", "group_done", "var_ready", "rstd_ready", "affine_ready"))
    dve_step, pool_step = sem("dve_step"), sem("pool_step")
    RES, INP = 0, 1
    lo, hi = slice(0, HALF), slice(HALF, P)

    def walk(eng, sample, chain=None, per_turn=0):
        sample(0)
        with eng.Fori(0, B - 2) as t:
            if chain:
                chain.turn(t, per_turn)
            sample(t + 1)
        if chain:
            chain.leave(B - 2)
        sample(B - 1)

    def pairs(ap):
        return ap.rearrange("p i (k e) -> p i k e", e=2)

    def table(which, b):
        return tab_k[:, which, b * 8:(b + 1) * 8, :].unsqueeze(3).to_broadcast([P, 8, J, 2])

    def angle(which, c):
        return tab_q[:, which, c * QR:(c + 1) * QR].unsqueeze(2).to_broadcast([P, QR, C])

    def bank_rows(ps):
        return ps[:, :].rearrange("p (h c) -> p h c", h=QR)

    def res_rows(c):
        return res[:, :, c * QR:(c + 1) * QR].rearrange("p c h -> p h c")

    def tap_views(t, c, out):
        kh, kw = t
        c0, c1 = (1 if kh == 0 else 0), (C - 1 if kh == 2 else C)
        return out[:, :, c0:c1], T[:, kw + c * QR:kw + (c + 1) * QR, c0 + kh - 1:c1 + kh - 1]

    first = lambda m: isinstance(m, int) and m == 0
    last = lambda m: isinstance(m, int) and m == B - 1

    with nc.Block() as block:

        @block.sync
        def _(sp):
            def load_x1(m):
                sp.dma_start(xr[:, :, :].rearrange("p i w -> p (i w)"),
                             x1[bass.ds(m * -1 + (B - 1), 1), :, :].rearrange("a p f -> (a p) f")).then_inc(x1_in, 16)

            def halves(ap, m):
                return [ap[bass.ds(m * -1 + (B - 1), 1)].rearrange("a c h w -> (a c) h w")[:, :, g * J:(g + 1) * J] for g in range(2)]

            def store_x2(m):
                sp.wait_ge(x2_ready, m + 1)
                for half in range(2):
                    sp.dma_start(x2[bass.ds(m * -1 + (B - 1), 1)].rearrange("a c (i q) w -> (a c) q i w", q=2)[:, half],
                                 xr[half * HALF:(half + 1) * HALF, :, :]).then_inc(x2_stored, 16)

            load_x1(0)
            store_x2(0)

            def sample(m):
                if not isinstance(m, int):
                    m = sp.snap(m)
                before = m * 32
                if not isinstance(m, int):
                    before = sp.snap(before)
                sp.wait_ge(x2_stored, before + 32)
                if not first(m):
                    sp.wait_ge(s_done, before)
                    sp.wait_ge(x3_stored, before)
                for g, src in enumerate(halves(x2, m)):
                    sp.dma_start(res[g * HALF:(g + 1) * HALF, :, :], src).then_inc(res_in, 16)
                if not last(m):
                    sp.wait_ge(g_ready, m + 1)
                    load_x1(m + 1)
                    store_x2(m + 1)
                sp.wait_ge(out_added, m * 4 + 4)
                for g, dst in enumerate(halves(x3, m)):
                    sp.dma_start(dst, res[g * HALF:(g + 1) * HALF, :, :]).then_inc(x3_stored, 16)

            walk(sp, sample)
            sp.wait_ge(x3_stored, 32 * B)

        @block.gpsimd
        def _(pool):
            chain = Chain(pool, pool_step)
            pool.dma_start(cst[:, :, :], consts).then_inc(consts_in, 16)
            for i, t in enumerate((cos_k, sin_k)):
                pool.dma_start(tab_k[:, i, :, :], t).then_inc(consts_in, 16)
            for i, t in enumerate((cos_q, sin_q)):
                pool.dma_start(tab_q[:, i, :], t).then_inc(consts_in, 16)
            pool.wait_ge(set_up, 2)
            for g in range(2):
                part = slice(g * HALF, (g + 1) * HALF)
                pool.dma_start(wq[part, part], wqk[:, 0:W]).then_inc(consts_in, 16)
                pool.dma_start(wk[part, part], wqk[:, W:2 * W]).then_inc(consts_in, 16)
                pool.dma_start(bq[part, :], bqk[0:W].rearrange("(c a) -> c a", a=1)).then_inc(consts_in, 16)
                pool.dma_start(lw[part, :], lepe_w).then_inc(consts_in, 16)
                pool.dma_start(lb[part, :], lepe_b.rearrange("(c a) -> c a", a=1)).then_inc(consts_in, 16)
            pool.dma_start(bk[:, :], bqk[W:2 * W].rearrange("(a k) -> a k", a=1).to_broadcast([P, W])).then_inc(consts_in, 16)

            def rstd(kind, r):
                pool.wait_ge(var_ready[kind], r + 1)
                c = slice(kind, kind + 1)
                newton_rsqrt(nc.gpsimd, chain, affine[:, 0, c], guess[:, c], var[:, c], three_halves[:, c], sq_pool[:, c], rstd_ready[kind])

            pool.wait_ge(consts_in, 16 * 16)
            pool.wait_ge(set_up, 7)
            rstd(INP, 0)

            def sample(m):
                for b in range(4):
                    pool.wait_ge(kk_ready, m * 4 + (b + 1))
                    wait_from(pool, kv_done, m * 4 + b)
                    wait_from(pool, out_added, m * 4)
                    nc.gpsimd.tensor_tensor(pairs(kcs[:, :, 1, :]), pairs(kt[b % 2][:, :, :]), table(1, b),
                                            ALU.mult).then_inc(ks_ready, 1)
                if not first(m):
                    rstd(RES, m - 1)
                for c in range(4):
                    g = m * 4 + c
                    pool.wait_ge(qq_ready, g + 1)
                    wait_from(pool, out_done, g)
                    nc.gpsimd.tensor_tensor(qs[:, :, :], qe[c % 2][:, :, :], angle(1, c), ALU.mult).then_inc(qs_ready, 1)
                    if c >= 1:
                        add_out(m, c - 1)
                add_out(m, 3)
                if not last(m):
                    rstd(INP, m + 1)

            def add_out(m, c):
                pool.wait_ge(out_scaled, m * 4 + (c + 1))
                pool.wait_ge(taps_done, m * 4 + (c + 1))
                nc.gpsimd.tensor_tensor(lepe[c % 2], lepe[c % 2], qr[c % 2][:, :, :], ALU.add).then_inc(both_ready, 1)

            walk(pool, sample, chain, 2 * NEWTON_STEPS)
            rstd(RES, B - 1)

        @block.scalar
        def _(act):
            def normalise(m):
                act.wait_ge(affine_ready[INP], m + 1)
                wait_from(act, kv_done, m * 4)
                nc.scalar.activation(G[:, :, :].rearrange("p (i g) w -> p g i w", g=2),
                                     xr[:, :, :].rearrange("p (g i) w -> p g i w", g=2), ACT.Identity, bias=affine[:, 1, INP:INP + 1],
                                     scale=affine[:, 0, INP:INP + 1]).then_inc(g_ready, 1)

            def sample(m):
                wait_from(act, q_done, m * 4)
                wait_from(act, lepe_done, m * 4)
                wait_from(act, taps_done, m * 4)
                for b in range(4):
                    act.wait_ge(tr_done, m * 4 + (b + 1))
                    nc.scalar.copy(T[:, 1 + 8 * b:9 + 8 * b, :], bank_rows(tk_ps[b % 2])).then_inc(t_ready, 1)
                act.wait_ge(t_ready, m * 6 + 4)
                nc.scalar.copy(T[hi, 0, :], T[lo, J, :]).then_inc(t_ready, 1)
                nc.scalar.copy(T[lo, J + 1, :], T[hi, 1, :]).then_inc(t_ready, 1)
                for b in range(4):
                    g = m * 4 + b
                    act.wait_ge(kt_ready, g + 1)
                    wait_from(act, kk_ready, g)
                    nc.scalar.activation(ke[:, :, :], kt[b % 2][:, :, :], ACT.Exp).then_inc(ke_ready, 1)
                    act.wait_ge(ke_ready, g + 1)
                    nc.scalar.activation(kt[b % 2][:, :, :], kt[b % 2][:, :, :], ACT.Relu).then_inc(kr_ready, 1)
                for c in range(4):
                    g = m * 4 + c
                    act.wait_ge(q_done, g + 1)
                    wait_from(act, z_done, g - 1)
                    wait_from(act, qs_ready, g - 1)
                    wait_from(act, both_ready, g - 1)
                    q = bank_rows(q_ps)
                    nc.scalar.activation(qe[c % 2][:, :, :], q, ACT.Exp, bias=bq).then_inc(qe_ready, 1)
                    nc.scalar.activation(qr[c % 2][:, :, :], q, ACT.Relu, bias=bq).then_inc(qr_ready, 1)
                    act.wait_ge(z_done, g + 1)
                    wait_from(act, out_scaled, g)
                    nc.scalar.activation(zs[:, :, :], bank_rows(z_ps), ACT.Identity,
                                         bias=eps_z).then_inc(zs_ready, 1)
                if not last(m):
                    normalise(m + 1)

            act.wait_ge(consts_in, 16 * 16)
            act.wait_ge(set_up, 7)
            normalise(0)
            walk(act, sample)

        @block.tensor
        def _(pe):
            def group(kind, r):
                pe.wait_ge(me_ready[kind], r + 1)
                nc.tensor.matmul(group_ps[:, kind, :], avg, me[:, kind, :], start=True, stop=True).then_inc(group_done[kind], 1)

            def kv(m, b):
                g = m * 4 + b
                pe.wait_ge(kc_ready, g + 1)
                pe.wait_ge(ks_ready, g + 1)
                for i in range(4):
                    nc.tensor.matmul(ksp_ps, kt[b % 2][:, 2 * i:2 * i + 2, :], ones[:, :],
                                     start=(b == 0 and i == 0), stop=(b == 3 and i == 3))
                for i in range(8):
                    mm = nc.tensor.matmul(ab_ps[:, 0:W], kcs[:, i, :, :], G[:, b * 8 + i, :],
                                          start=(b == 0 and i == 0), stop=(b == 3 and i == 7))
                mm.then_inc(kv_done, 1)

            def q_chunk(m, c):
                pe.wait_ge(t_ready, m * 6 + 6)
                g = m * 4 + c
                wait_from(pe, qr_ready, g)
                nc.tensor.matmul(q_ps[:, :], wq[:, :], T[:, 1 + c * QR:1 + (c + 1) * QR, :],
                                 start=True, stop=True).then_inc(q_done, 1)
                wait_from(pe, lepe_added, g)
                for i, t in enumerate(PE_TAPS):
                    out, x = tap_views(t, c, bank_rows(lepe_ps))
                    mm = nc.tensor.matmul(out, diag[:, i, :], x, start=(i == 0), stop=(i == len(PE_TAPS) - 1))
                mm.then_inc(lepe_done, 1)

            def sample(m):
                pe.wait_ge(g_ready, m + 1)
                for b in range(4):
                    if b >= 2:
                        pe.wait_ge(t_ready, m * 6 + (b - 1))
                    for i in range(4):
                        row = b * 8 + i * 2
                        mm = nc.tensor.transpose(tk_ps[b % 2][:, i * P:(i + 1) * P], G[:, row:row + 2, :], ident)
                    mm.then_inc(tr_done, 1)
                for b in range(4):
                    pe.wait_ge(t_ready, m * 6 + (3 + b if b < 2 else 4))
                    if b >= 2:
                        pe.wait_ge(kt_ready, m * 4 + (b - 1))
                    for i in range(4):
                        row = b * 8 + i * 2
                        mm = nc.tensor.matmul(tk_ps[b % 2][:, i * P:(i + 1) * P],
                                              T[:, 1 + row:3 + row, :], wk[:, :],
                                              start=True, stop=True)
                    mm.then_inc(k_done, 1)
                    if b >= 1:
                        kv(m, b - 1)
                kv(m, 3)
                if not first(m):
                    group(RES, m - 1)
                q_chunk(m, 0)
                pe.wait_ge(ab_ready, m + 1)
                nc.tensor.matmul(rot_ps[0], rot1, ab[:, :], start=True, stop=True)
                nc.tensor.matmul(rot_ps[1], rot2, ab[:, :], start=True, stop=True)
                nc.tensor.matmul(ks_ps, same_j, ks, start=True, stop=True).then_inc(rot_done, 1)
                for c in range(4):
                    g = m * 4 + c
                    if c < 3:
                        q_chunk(m, c + 1)
                    if c == 0:
                        pe.wait_ge(kvw_ready, m * 3 + 3)
                    pe.wait_ge(qq_ready, g + 1)
                    wait_from(pe, zs_ready, g)
                    nc.tensor.matmul(z_ps[:, :], kvw[:, 2, :], qe[c % 2][:, :, :], start=True, stop=True).then_inc(z_done, 1)
                    pe.wait_ge(qc_ready, g + 1)
                    pe.wait_ge(qs_ready, g + 1)
                    wait_from(pe, out_scaled, g)
                    nc.tensor.matmul(out_ps[:, :], kvw[:, 0, :], qr[c % 2][:, :, :], start=True, stop=False)
                    nc.tensor.matmul(out_ps[:, :], kvw[:, 1, :], qs[:, :, :], start=False, stop=True).then_inc(out_done, 1)
                if not last(m):
                    group(INP, m + 1)

            pe.wait_ge(consts_in, 16 * 16)
            pe.wait_ge(set_up, 7 + len(PE_TAPS))
            group(INP, 0)
            walk(pe, sample)
            group(RES, B - 1)

        @block.vector
        def _(dve):
            chain = Chain(dve, dve_step)

            def stats(kind, x, flat):
                for q in range(4):
                    nc.vector.bn_stats(bn[:, kind, q, :], flat(x, q)).then_inc(dve_step, 1)
                    chain.count += 1
                dve.wait_ge(dve_step, chain.offset + chain.count)
                c = slice(kind, kind + 1)
                chain.carry(pause)
                chain.step(nc.vector.bn_aggr(mv[:, kind, :], bn[:, kind, :, :]))
                chain.step(nc.vector.tensor_tensor(sq[:, c], mv[:, c, 0], mv[:, c, 0], ALU.mult))
                nc.vector.tensor_copy(me[:, c, 0], mv[:, c, 0])
                nc.vector.tensor_tensor(me[:, c, 1], sq[:, c], mv[:, c, 1], ALU.add).then_inc(me_ready[kind], 1)

            def group_var(kind, r):
                c = slice(kind, kind + 1)
                dve.wait_ge(group_done[kind], r + 1)
                chain.step(nc.vector.tensor_copy(gs[:, c, :], group_ps[:, c, :]))
                chain.step(nc.vector.tensor_tensor(sq[:, c], gs[:, c, 0], gs[:, c, 0], ALU.mult))
                chain.step(nc.vector.scalar_tensor_tensor(out=var[:, c], in0=gs[:, c, 1], scalar=GN_EPS, in1=sq[:, c],
                                                          op0=ALU.add, op1=ALU.subtract))
                rsqrt_guess(nc, chain, guess[:, c], sq[:, c], var[:, c]).then_inc(var_ready[kind], 1)

            def group_affine(kind, r):
                c = slice(kind, kind + 1)
                dve.wait_ge(rstd_ready[kind], r + 1)
                nc.vector.scalar_tensor_tensor(out=affine[:, 1, c], in0=gs[:, c, 0], scalar=-1.0,
                                               in1=affine[:, 0, c], op0=ALU.mult, op1=ALU.mult).then_inc(affine_ready[kind], 1)

            def input_part(m):
                dve.wait_ge(x1_in, m * 16 + 16)
                nc.vector.tensor_tensor(xr[:, :, :], xr[:, :, :],
                                        S[:, bass.ds(m * -1 + (B - 1), 1), :, :].rearrange("p a w i -> p i (a w)"),
                                        ALU.add).then_inc(x2_ready, 1)
                dve.wait_ge(x2_ready, m + 1)
                stats(INP, xr, lambda x, q: x[:, q * 8:(q + 1) * 8, :].rearrange("p i w -> p (i w)"))

            def result_stats(m):
                dve.wait_ge(out_added, m * 4 + 4)
                stats(RES, res, lambda x, q: x[:, q * 16:(q + 1) * 16, :].rearrange("p i w -> p (i w)"))

            def to_slot(m):
                group_affine(RES, m)
                dve.wait_ge(affine_ready[RES], m + 1)
                for g, part in enumerate((lo, hi)):
                    for pw in range(2):
                        dst = S[pw * HALF:(pw + 1) * HALF, bass.ds(m * -1 + B, 1), :, g * 16:(g + 1) * 16].rearrange(
                            "p a h w -> p (a h) w")
                        src = res[part, :, :].rearrange("p c (w q) -> p q c w", q=2)[:, pw]
                        nc.vector.tensor_scalar(dst, src, affine[part, 0, RES:RES + 1], affine[part, 1, RES:RES + 1],
                                                ALU.mult, ALU.add).then_inc(s_done, 8)

            def k_bias(m, b):
                g = m * 4 + b
                dve.wait_ge(k_done, g + 1)
                wait_from(dve, kv_done, g - 1)
                nc.vector.tensor_tensor(kt[b % 2][:, :, :], tk_ps[b % 2][:, :].rearrange("p (i j) -> p i j", i=8),
                                        bk[:, :].unsqueeze(1).to_broadcast([P, 8, W]), ALU.add).then_inc(kt_ready, 1)

            def k_finish(m, b):
                g = m * 4 + b
                k = kt[b % 2]
                dve.wait_ge(kr_ready, g + 1)
                nc.vector.scalar_tensor_tensor(out=k[:, :, :], in0=ke[:, :, :], scalar=1.0, in1=k[:, :, :],
                                               op0=ALU.min, op1=ALU.add).then_inc(kk_ready, 1)
                dve.wait_ge(kk_ready, g + 1)
                wait_from(dve, kv_done, g)
                wait_from(dve, out_added, m * 4)
                nc.vector.tensor_tensor(pairs(kcs[:, :, 0, :]), pairs(k[:, :, :]), table(0, b), ALU.mult).then_inc(kc_ready, 1)

            def q_finish(m, c):
                g = m * 4 + c
                q = qe[c % 2]
                dve.wait_ge(qr_ready, g + 1)
                nc.vector.scalar_tensor_tensor(out=q[:, :, :], in0=q[:, :, :], scalar=1.0, in1=qr[c % 2][:, :, :],
                                               op0=ALU.min, op1=ALU.add).then_inc(qq_ready, 1)
                dve.wait_ge(qq_ready, g + 1)
                nc.vector.tensor_tensor(qr[c % 2][:, :, :], q[:, :, :], angle(0, c), ALU.mult).then_inc(qc_ready, 1)

            def scale_out(m, c):
                g = m * 4 + c
                dve.wait_ge(zs_ready, g + 1)
                chain.step(nc.vector.reciprocal(zs[:, :, :], zs[:, :, :]))
                dve.wait_ge(out_done, g + 1)
                nc.vector.tensor_tensor(qr[c % 2][:, :, :], bank_rows(out_ps), zs[:, :, :],
                                        ALU.mult).then_inc(out_scaled, 1)

            def taps(m, c):
                g = m * 4 + c
                dve.wait_ge(lepe_done, g + 1)
                wait_from(dve, out_added, g - 1)
                for i, t in enumerate(DVE_TAPS):
                    out, x = tap_views(t, c, lepe[c % 2])
                    w = lw[:, 3 * t[0] + t[1]:3 * t[0] + t[1] + 1]
                    so_far = bank_rows(lepe_ps) if i == 0 else out
                    tap = nc.vector.scalar_tensor_tensor(out=out, in0=x, scalar=w, in1=so_far, op0=ALU.mult, op1=ALU.add)
                    if i == 0:
                        tap.then_inc(lepe_added, 1)
                        dve.wait_ge(lepe_added, g + 1)
                    elif i < len(DVE_TAPS) - 1:
                        chain.step(tap)
                tap.then_inc(taps_done, 1)

            def to_result(m, c):
                if c == 0:
                    dve.wait_ge(res_in, m * 32 + 32)
                dve.wait_ge(both_ready, m * 4 + (c + 1))
                nc.vector.scalar_tensor_tensor(out=res_rows(c), in0=lepe[c % 2], scalar=lb, in1=res_rows(c),
                                               op0=ALU.add, op1=ALU.add).then_inc(out_added, 1)

            def sample(m):
                if not first(m):
                    result_stats(m - 1)
                for b in range(4):
                    k_bias(m, b)
                    if b >= 1:
                        k_finish(m, b - 1)
                k_finish(m, 3)
                if not first(m):
                    group_var(RES, m - 1)
                dve.wait_ge(kv_done, m * 4 + 4)
                chain.step(nc.vector.tensor_copy(ks, ksp_ps))
                nc.vector.tensor_copy(ab[:, :], ab_ps[:, 0:W]).then_inc(ab_ready, 1)
                dve.wait_ge(rot_done, m + 1)
                for i in range(2):
                    nc.vector.tensor_tensor(kvw[:, i, :].rearrange("p (g e) -> p g e", g=2),
                                            rot_ps[i].unsqueeze(1).to_broadcast([P, 2, W]),
                                            mask.rearrange("p (g e) -> p g e", g=2), ALU.mult).then_inc(kvw_ready, 1)
                chain.step(nc.vector.tensor_copy(ks, ks_ps))
                nc.vector.tensor_scalar(kvw[:, 2, :], mask, ks, None, ALU.mult).then_inc(kvw_ready, 1)
                if not first(m):
                    to_slot(m - 1)
                if not last(m):
                    input_part(m + 1)
                for c in range(4):
                    q_finish(m, c)
                    if c >= 1:
                        scale_out(m, c - 1)
                    if c >= 2:
                        to_result(m, c - 2)
                    taps(m, c)
                scale_out(m, 3)
                to_result(m, 2)
                to_result(m, 3)
                if not last(m):
                    group_var(INP, m + 1)
                    group_affine(INP, m + 1)

            nc.vector.memset(wq[:, :], 0.0).then_inc(set_up, 1)
            nc.vector.memset(wk[:, :], 0.0).then_inc(set_up, 1)
            nc.vector.memset(T[:, :, :], 0.0).then_inc(set_up, 1)
            nc.vector.memset(ones[:, :], 1.0).then_inc(set_up, 1)
            nc.vector.memset(three_halves, 1.5).then_inc(set_up, 1)
            nc.vector.memset(pause, 1.0).then_inc(set_up, 1)
            nc.vector.memset(eps_z, 1e-6).then_inc(set_up, 1)
            dve.wait_ge(consts_in, 16 * 16)
            for i, t in enumerate(PE_TAPS):
                w = lw[:, 3 * t[0] + t[1]:3 * t[0] + t[1] + 1]
                nc.vector.tensor_scalar(diag[:, i, :], ident, w, None, ALU.mult).then_inc(set_up, 1)
            input_part(0)
            group_var(INP, 0)
            group_affine(INP, 0)
            walk(dve, sample, chain, AT_LOOP)
            result_stats(B - 1)
            group_var(RES, B - 1)
            to_slot(B - 1)


AT_LOOP = 42


def attention_constants():
    import numpy as np
    p = np.arange(P)
    j, g = p % HALF, p // HALF
    avg = (j[:, None] // 2 == j[None] // 2) * 0.25
    ident = np.eye(P)
    mask = (g[:, None] == g[None]) * (j[:, None] // HD == j[None] // HD) / float(H * W)
    rot1, rot2 = np.zeros((P, P)), np.zeros((P, P))
    for d in range(W):
        for out in (d, d + HALF):
            even = d % 2 == 0
            other = d + 1 if even else d - 1
            rot1[d, out] = 1
            rot1[HALF + other, out] = -1 if even else 1
            rot2[other, out] = 1 if even else -1
            rot2[HALF + d, out] = 1
    same_j = j[:, None] == j[None]
    mats = np.stack([avg, ident, mask, rot1, rot2, same_j], 1).astype(np.float32)
    theta = (1.0 / np.float32(10000.0) ** (np.arange(W // 2, dtype=np.float32) / np.float32(W // 2))).astype(np.float32)
    angles = np.arange(H, dtype=np.float32)[:, None] * theta
    i, gg = np.arange(J) // 2, np.arange(J) % 2
    h_k = 2 * (i + 16 * gg)[None, :] + g[:, None]
    h_q = 32 * g[:, None] + np.arange(J)[None, :]
    ak = angles[h_k]
    aq = angles[h_q, (j // 2)[:, None]]
    f = lambda a: np.ascontiguousarray(a.astype(np.float32))
    return f(mats), f(np.cos(ak)), f(np.sin(ak)), f(np.cos(aq)), f(np.sin(aq))


def final_sum(nc, ctx, S, x3, out):
    BUFS = 4
    buf = [ctx.enter_context(nc.sbuf_tensor(f"fs_buf{u}", [P, J, W], F32)) for u in range(BUFS)]
    sem = semaphores(nc, ctx, "fs")
    loaded = [sem(f"loaded{u}") for u in range(BUFS)]
    stored = [sem(f"stored{u}") for u in range(BUFS)]
    added = sem("added")

    def half_of(ap, n, half):
        return ap[bass.ds(n, 1)].rearrange("a c (i q) w -> (a c) q i w", q=2)[:, half]

    with nc.Block() as block:

        @block.sync
        def _(sp):
            def load(n, u):
                for half in range(2):
                    sp.dma_start(buf[u][half * HALF:(half + 1) * HALF, :, :], half_of(x3, n, half)).then_inc(loaded[u], 16)

            for n in range(BUFS):
                load(n, n)
            with sp.Fori(0, B // BUFS - 1) as t:
                for u in range(BUFS):
                    sp.wait_ge(stored[u], t * 32 + 32)
                    load(t * BUFS + (u + BUFS), u)

        @block.scalar
        def _(act):
            with act.Fori(0, B // BUFS) as t:
                for u in range(BUFS):
                    n = t * BUFS + u
                    act.wait_ge(loaded[u], t * 32 + 32)
                    act.wait_ge(added, n + 1)
                    for half in range(2):
                        act.dma_start(half_of(out, n, half), buf[u][half * HALF:(half + 1) * HALF, :, :]).then_inc(stored[u], 16)
            for u in range(BUFS):
                act.wait_ge(stored[u], 32 * (B // BUFS))

        @block.vector
        def _(dve):
            with dve.Fori(0, B // BUFS) as t:
                for u in range(BUFS):
                    n = t * BUFS + u
                    dve.wait_ge(loaded[u], t * 32 + 32)
                    nc.vector.tensor_tensor(buf[u][:, :, :], buf[u][:, :, :],
                                            S[:, bass.ds(n, 1), :, :].rearrange("p a w i -> p i (a w)"),
                                            ALU.add).then_inc(added, 1)


def build(nc, a, out):
    x1 = nc.dram_tensor("x1_scratch", [B, P, J * W], F32, kind="Internal").ap()
    x2 = nc.dram_tensor("x2_scratch", [B, C, H, W], F32, kind="Internal").ap()
    x3 = nc.dram_tensor("x3_scratch", [B, C, H, W], F32, kind="Internal").ap()
    with ExitStack() as whole:
        S = whole.enter_context(nc.sbuf_tensor("S", [P, B + 1, H, J], F32))

        def scnn(layer):
            for first, second, base in (("d", "u", 1), ("r", "l", 0)):
                with ExitStack() as ctx:
                    names = [f"L{layer}_conv_{{}}_{k}" for k in (first, second)]
                    sweep_pair(nc, ctx, S, base, [a[n.format("w")] for n in names], [a[n.format("b")] for n in names],
                               f"L{layer}{first}{second}")
                if base:
                    with ExitStack() as ctx:
                        relayout(nc, ctx, S, f"L{layer}re")

        with ExitStack() as ctx:
            dyn_conv(nc, ctx, S, a["x"], x1, a["L0_conv_experts"], a["L0_conv_bias"], a["L0_conv_w1"], a["L0_conv_b1"],
                     a["L0_conv_w2"], a["L0_conv_b2"], a["group_avg"])
        scnn(1)
        with ExitStack() as ctx:
            attention(nc, ctx, S, x1, x2, x3, a["matrices"], a["cos_k"], a["sin_k"], a["cos_q"], a["sin_q"],
                      a["L2_conv_qk_w"], a["L2_conv_qk_b"], a["L2_conv_lepe_w"], a["L2_conv_lepe_b"])
        scnn(3)
        with ExitStack() as ctx:
            final_sum(nc, ctx, S, x3, out)


def lay_out(inputs):
    import numpy as np
    a = {k: np.asarray(v) for k, v in inputs.items()}
    a["x"] = a["x"].reshape(B, C, J, 2, W)
    a["L0_conv_experts"] = a["L0_conv_experts"].transpose(2, 0, 3, 4, 1)
    for name in ("L0_conv_bias", "L0_conv_w1", "L0_conv_w2", "L2_conv_qk_w"):
        a[name] = a[name].T
    for layer in (1, 3):
        for k in "durl":
            a[f"L{layer}_conv_w_{k}"] = a[f"L{layer}_conv_w_{k}"].transpose(1, 2, 0)
    a["L2_conv_lepe_w"] = a["L2_conv_lepe_w"].reshape(C, 9)
    a["matrices"], a["cos_k"], a["sin_k"], a["cos_q"], a["sin_q"] = attention_constants()
    a["group_avg"] = a["matrices"][:, 0, :]
    return {k: np.ascontiguousarray(v) for k, v in a.items()}


def kernel(**inputs):
    import concourse.bacc as bacc
    from concourse.bass_utils import run_bass_kernel_spmd

    nc = bacc.Bacc("TRN2", target_bir_lowering=False, num_devices=1)
    arrays = lay_out(inputs)
    aps = {k: nc.dram_tensor(k, v.shape, mybir.dt.from_np(v.dtype), kind="ExternalInput").ap() for k, v in arrays.items()}
    out = nc.dram_tensor("out", [B, C, H, W], F32, kind="ExternalOutput").ap()
    build(nc, aps, out)
    result = run_bass_kernel_spmd(nc, [arrays], core_ids=[0])
    return result.results[0]["out"]
```

```python
from contextlib import ExitStack

import concourse.bass as bass
from concourse import mybir

P = 128
B, C, H, W = 16, 64, 64, 64
HALF = 64
J = 32
GROUPS = 32
KTAPS = 9
NBLK = 5
NB = B // 2
PADJ = 2
STEPS = 63

F32 = mybir.dt.float32
F32R = mybir.dt.float32r
I32 = mybir.dt.int32
ALU = mybir.AluOpType
ACT = mybir.ActivationFunctionType
AX_X = mybir.AxisListType.X


def semaphores(nc, ctx, tag):
    taken = []

    def sem(name):
        taken.append(nc.alloc_semaphore(name=f"{tag}_{name}"))
        return taken[-1]

    def clear():
        nc.clear_and_free_semaphores(taken)
        nc.all_engine_barrier()

    ctx.callback(clear)
    return sem


def sweep_pair(nc, ctx, S, base, w_taps, biases, tag):
    def sb(name, shape, dt=F32):
        return ctx.enter_context(nc.sbuf_tensor(f"{tag}_{name}", shape, dt))

    sem = semaphores(nc, ctx, tag)

    w_raw = sb("w_raw", [P, 2, NBLK * P])
    w_hi = sb("w_hi", [P, 2, NBLK * P], F32R)
    w_lo = sb("w_lo", [P, 2, NBLK * P], F32R)
    bias = sb("bias", [P, 2])
    neg_bias = sb("neg_bias", [P, 2])
    row_b = [sb(f"row_b{p}", [P, NB, J]) for p in range(2)]
    x_hi = [sb(f"x_hi{p}", [P, NB, J + 2 * PADJ], F32R) for p in range(2)]
    x_lo = [sb(f"x_lo{p}", [P, NB, J + 2 * PADJ], F32R) for p in range(2)]
    conv = [ctx.enter_context(nc.psum_tensor(f"{tag}_conv{p}", [P, 512], F32)) for p in range(2)]

    w_zeroed = sem("w_zeroed")
    w_loaded = sem("w_loaded")
    b_loaded = sem("b_loaded")
    b_ready = sem("b_ready")
    w_hi_ready = sem("w_hi_ready")
    w_ready = sem("w_ready")
    pads_ready = sem("pads_ready")
    row_b_ready = [sem(f"row_b_ready{p}") for p in range(2)]
    conv_done = [sem(f"conv_done{p}") for p in range(2)]
    new_ready = [sem(f"new_ready{p}") for p in range(2)]
    hi_ready = [sem(f"hi_ready{p}") for p in range(2)]
    lo_ready = [sem(f"lo_ready{p}") for p in range(2)]

    def slots(p):
        return slice(base + p * NB, base + (p + 1) * NB)

    with nc.Block() as block:

        @block.sync
        def _(sp):
            sp.wait_ge(w_zeroed, 1)
            for k in range(2):
                blocks = w_raw[:, k, :].rearrange("p (s o c) -> p s o c", s=NBLK, o=2)
                for pi in range(2):
                    for po in range(2):
                        s0 = 1 if pi < po else 0
                        s1 = NBLK - 1 if pi > po else NBLK
                        t0 = 2 * s0 + pi - po
                        sp.dma_start(blocks[pi * HALF:(pi + 1) * HALF, s0:s1, po, :],
                                     w_taps[k][:, t0:t0 + 2 * (s1 - s0) - 1:2, :]).then_inc(w_loaded, 16)

        @block.gpsimd
        def _(pool):
            for k in range(2):
                for half in range(2):
                    pool.dma_start(bias[half * HALF:(half + 1) * HALF, k:k + 1],
                                   biases[k].rearrange("(c a) -> c a", a=1)).then_inc(b_loaded, 16)

        @block.scalar
        def _(act):
            act.wait_ge(b_loaded, 64)
            for k in range(2):
                with act.Fori(0, STEPS) as i:
                    row = act.snap(i + 1 if k == 0 else i * -1 + (STEPS - 1))
                    step = act.snap(i + (k * STEPS + 1))
                    for p in range(2):
                        act.wait_ge(hi_ready[p], step)
                        nc.scalar.activation(row_b[p][:, :, :], S[:, slots(p), bass.ds(row, 1), :],
                                             ACT.Identity, bias=bias[:, k:k + 1]).then_inc(row_b_ready[p], 1)

        @block.vector
        def _(dve):
            nc.vector.memset(w_raw[:, :, :], 0.0).then_inc(w_zeroed, 1)
            for p in range(2):
                nc.vector.memset(x_hi[p][:, :, :].bitcast(F32), 0.0).then_inc(pads_ready, 1)
                nc.vector.memset(x_lo[p][:, :, :].bitcast(F32), 0.0).then_inc(pads_ready, 1)
            dve.wait_ge(b_loaded, 64)
            nc.vector.tensor_scalar_mul(neg_bias[:, :], bias[:, :], -1.0).then_inc(b_ready, 1)
            dve.wait_ge(pads_ready, 4)
            for p in range(2):
                nc.vector.tensor_copy(x_hi[p][:, :, PADJ:PADJ + J], S[:, slots(p), 0, :]).then_inc(hi_ready[p], 1)
                dve.wait_ge(hi_ready[p], 1)
                nc.vector.tensor_tensor(x_lo[p][:, :, PADJ:PADJ + J], S[:, slots(p), 0, :],
                                        x_hi[p][:, :, PADJ:PADJ + J].bitcast(F32), ALU.subtract).then_inc(lo_ready[p], 1)
            dve.wait_ge(w_loaded, 8 * 16)
            nc.vector.tensor_copy(w_hi[:, :, :], w_raw[:, :, :]).then_inc(w_hi_ready, 1)
            dve.wait_ge(w_hi_ready, 1)
            nc.vector.tensor_tensor(w_lo[:, :, :], w_raw[:, :, :], w_hi[:, :, :].bitcast(F32),
                                    ALU.subtract).then_inc(w_ready, 1)
            dve.wait_ge(b_ready, 1)
            for k in range(2):
                with dve.Fori(0, STEPS) as i:
                    row = dve.snap(i + 1 if k == 0 else i * -1 + (STEPS - 1))
                    step = dve.snap(i + (k * STEPS + 1))
                    for p in range(2):
                        new = S[:, slots(p), bass.ds(row, 1), :]
                        dve.wait_ge(row_b_ready[p], step)
                        dve.wait_ge(conv_done[p], step)
                        nc.vector.scalar_tensor_tensor(
                            out=new, in0=conv[p][:, 0:NB * J].rearrange("p (b j) -> p b j", b=NB),
                            scalar=neg_bias[:, k:k + 1], in1=row_b[p][:, :, :],
                            op0=ALU.max, op1=ALU.add).then_inc(new_ready[p], 1)
                        dve.wait_ge(new_ready[p], step)
                        nc.vector.tensor_scalar(x_hi[p][:, :, PADJ:PADJ + J], new, 1.0, None, ALU.mult).then_inc(hi_ready[p], 1)
                        dve.wait_ge(hi_ready[p], step + 1)
                        nc.vector.tensor_tensor(x_lo[p][:, :, PADJ:PADJ + J], new,
                                                x_hi[p][:, :, PADJ:PADJ + J].bitcast(F32),
                                                ALU.subtract).then_inc(lo_ready[p], 1)

        @block.tensor
        def _(pe):
            pe.wait_ge(w_ready, 1)
            for k in range(2):
                with pe.Fori(0, STEPS) as i:
                    step = pe.snap(i + (k * STEPS + 1))
                    for p in range(2):
                        out = conv[p][:, 0:NB * J]
                        pe.wait_ge(hi_ready[p], step)
                        for s in range(NBLK):
                            for n, w in enumerate((w_hi, w_lo)):
                                nc.tensor.matmul(out, w[:, k, s * P:(s + 1) * P], x_hi[p][:, :, s:s + J],
                                                 start=(s == 0 and n == 0), stop=False)
                        pe.wait_ge(lo_ready[p], step)
                        for s in range(NBLK):
                            mm = nc.tensor.matmul(out, w_hi[:, k, s * P:(s + 1) * P], x_lo[p][:, :, s:s + J],
                                                  start=False, stop=(s == NBLK - 1))
                        mm.then_inc(conv_done[p], 1)


def relayout(nc, ctx, S, tag):
    sem = semaphores(nc, ctx, tag)
    moved = [sem(f"moved_{e}") for e in ("dve", "act")]

    def quarter(b, pw, ph):
        src = S[pw * HALF:(pw + 1) * HALF, bass.ds(b + 1, 1), :, :].rearrange("p a (h q) w -> p (a q) h w", q=2)[:, ph]
        dst = S[ph * HALF:(ph + 1) * HALF, bass.ds(b, 1), :, :].rearrange("p a (w q) h -> p (a q) h w", q=2)[:, pw]
        return dst, src

    with nc.Block() as block:
        @block.vector
        def _(dve):
            with dve.Fori(0, B) as b:
                for pw in range(2):
                    nc.vector.tensor_copy(*quarter(b, pw, 0)).then_inc(moved[0], 1)
                done = dve.snap(b * 2 + 2)
                dve.wait_ge(moved[0], done)
                dve.wait_ge(moved[1], done)

        @block.scalar
        def _(act):
            with act.Fori(0, B) as b:
                for pw in range(2):
                    nc.scalar.copy(*quarter(b, pw, 1)).then_inc(moved[1], 1)
                done = act.snap(b * 2 + 2)
                act.wait_ge(moved[0], done)
                act.wait_ge(moved[1], done)


def wait_from(eng, sem, value):
    if not isinstance(value, int) or value > 0:
        eng.wait_ge(sem, value)


CH = 4
CB = J // CH
WP = W + 2
KE = 4
HID = 32
PER_LOOP = 29
XN = [4, 7, 10, 14]
PER = 4
TURNS = 3
GN_EPS = 1e-5


class Chain:

    def __init__(self, eng, sem):
        self.eng, self.sem, self.count, self.offset = eng, sem, 0, 0

    def step(self, instruction):
        instruction.then_inc(self.sem, 1)
        self.count += 1
        self.eng.wait_ge(self.sem, self.offset + self.count)

    def carry(self, pause):
        self.eng.tensor_tensor(pause, pause, pause, ALU.mult).then_inc(self.sem, 1)
        self.count += 1

    def turn(self, t, per_turn):
        self.offset, self.per_turn, self.start = t * per_turn, per_turn, self.count

    def leave(self, turns):
        assert self.count - self.start == self.per_turn, self.count - self.start
        self.count += (turns - 1) * self.per_turn
        self.offset = 0


NEWTON_STEPS = 11


def newton_rsqrt(eng, chain, out, guess, half_var, one_half, tmp, ready):
    for i in range(3):
        chain.step(eng.tensor_tensor(tmp, guess, guess, ALU.mult))
        chain.step(eng.tensor_tensor(tmp, tmp, half_var, ALU.mult))
        chain.step(eng.tensor_tensor(tmp, one_half, tmp, ALU.subtract))
        if i < 2:
            chain.step(eng.tensor_tensor(guess, guess, tmp, ALU.mult))
    eng.tensor_tensor(out, guess, tmp, ALU.mult).then_inc(ready, 1)


def rsqrt_guess(nc, chain, guess, half, var):
    chain.step(nc.vector.tensor_scalar(half.bitcast(I32), var.bitcast(I32), 1, None, ALU.logical_shift_right))
    chain.step(nc.vector.tensor_scalar(var, var, 0.5, None, ALU.mult))
    return nc.vector.tensor_scalar(guess.bitcast(I32), half.bitcast(I32), -1.0, float(0x5f3759df), ALU.mult, ALU.add)


def dyn_conv(nc, ctx, S, x_in, x1_out, experts, bias_k, w1, b1, w2, b2, group_avg):
    def sb(name, shape, dt=F32):
        return ctx.enter_context(nc.sbuf_tensor(f"dc_{name}", shape, dt))

    sem = semaphores(nc, ctx, "dc")

    raw = [sb(f"raw{u}", [P, J, W]) for u in range(PER)]
    xn = S[:, 0, :, :].rearrange("p a b -> p (a b)").rearrange("p (u m i w) -> p u m i w", u=2, m=2, i=CB)
    xz_hi = [sb(f"xz_hi{u}", [P, 2, CB, WP], F32R) for u in range(2)]
    xz_lo = [sb(f"xz_lo{u}", [P, 2, CB, WP], F32R) for u in range(2)]
    ex = sb("ex", [P, KE, 2 * 3, P])
    w_mix = sb("w_mix", [P, 2 * 3, P])
    w_hi = sb("w_hi", [P, 2 * 3, P], F32R)
    w_lo = sb("w_lo", [P, 2 * 3, P], F32R)
    avg = sb("avg", [P, P])
    ones = sb("ones", [HID, P])
    w1s = sb("w1s", [P, HID])
    zeros = sb("zeros", [P, W])
    bn = sb("bn", [P, 2, CH, 6])
    small = sb("small", [P, 72])
    pause = small[:, 70:71]
    b1s, h, w2s, w2h = small[0:HID, 0:1], small[0:HID, 1:2], small[0:HID, 4:8], small[0:HID, 8:12]
    b2s, bks = small[:, 12:16], small[:, 16:20]
    logit, prob, alpha, bprod = small[:, 20:24], small[:, 24:28], small[:, 28:32], small[:, 32:36]
    top, total, beff, gmean = small[:, 36:37], small[:, 37:38], small[:, 38:39], small[:, 39:40]
    stat = [small[:, 40 + 4 * i:44 + 4 * i].rearrange("p (a b) -> p a b", a=2) for i in range(3)]
    mv, me, gs = stat
    sq = small[:, 52:54]
    var = small[:, 54:56]
    guess, sq_pool, three_halves = small[:, 64:66], small[:, 66:68], small[:, 68:70]
    affine = [small[:, 56 + 4 * u:60 + 4 * u].rearrange("p (b a) -> p b a", b=2) for u in range(2)]

    conv = [ctx.enter_context(nc.psum_tensor(f"dc_conv{u}", [P, 512], F32)) for u in range(2)]
    tiny = ctx.enter_context(nc.psum_tensor("dc_tiny", [P, 512], F32))
    hid_ps, logit_ps = tiny[0:HID, 8:9], tiny[:, 16:16 + KE]
    group_ps = tiny[:, 0:4].rearrange("p (a b) -> p a b", a=2)

    consts_in, ex_zeroed, ex_in, set_up = sem("consts_in"), sem("ex_zeroed"), sem("ex_in"), sem("set_up")
    raw_in = [sem(f"raw_in{u}") for u in range(PER)]
    x1_stored, s_done = sem("x1_stored"), sem("s_done")
    xn_ready, hi_ready, lo_ready = sem("xn_ready"), sem("hi_ready"), sem("lo_ready")
    conv_done, evac_done, w_ready = sem("conv_done"), sem("evac_done"), sem("w_ready")
    me_ready, group_done, var_ready = sem("me_ready"), sem("group_done"), sem("var_ready")
    rstd_ready, affine_ready, gmean_ready = sem("rstd_ready"), sem("affine_ready"), sem("gmean_ready")
    hid_done, h_ready, w2h_ready = sem("hid_done"), sem("h_ready"), sem("w2h_ready")
    logit_done, logit_ready, prob_ready = sem("logit_done"), sem("logit_ready"), sem("prob_ready")
    dve_step, pool_step = sem("dve_step"), sem("pool_step")
    RES, INP, BOTH = slice(0, 1), slice(1, 2), slice(0, 2)

    def chunk(t, q):
        return t[:, q * CB:(q + 1) * CB, :].rearrange("p i w -> p (i w)")

    def slot_move(n, u, parity, ph, pw):
        part = slice(ph * HALF, (ph + 1) * HALF)
        dst = S[pw * HALF:(pw + 1) * HALF, bass.ds(n + 1, 1), :, :].rearrange("p a (h q) w -> p (a q) h w", q=2)[:, ph]
        src = raw[u][part, :, :].rearrange("p i (w q) -> p q i w", q=2)[:, pw]
        return dst, src, affine[parity][part, 0, RES], affine[parity][part, 1, RES]

    def cols(n):
        return INP if isinstance(n, int) and n == 0 else RES if isinstance(n, int) and n == B - 1 else BOTH

    def walk(eng, sample, chain=None, per_turn=0):
        sample(0, 0)
        sample(0, 1)
        with eng.Fori(0, TURNS) as t:
            if chain:
                chain.turn(t, per_turn)
            for k in range(2, 2 + PER):
                sample(t, k)
        if chain:
            chain.leave(TURNS)
        sample(TURNS, 2)
        sample(TURNS, 3)

    with nc.Block() as block:

        @block.sync
        def _(sp):
            def load(n, u):
                for half in range(2):
                    sp.dma_start(raw[u][half * HALF:(half + 1) * HALF, :, :],
                                 x_in[bass.ds(n, 1), :, :, half, :].rearrange("a c i w -> (a c) i w")
                                 ).then_inc(raw_in[u], 16)

            def store(n, u):
                sp.wait_ge(evac_done, n * CH + CH)
                sp.dma_start(x1_out[bass.ds(n, 1), :, :].rearrange("a p f -> (a p) f"),
                             raw[u][:, :, :].rearrange("p i w -> p (i w)")).then_inc(x1_stored, 16)

            for n in range(PER):
                load(n, n)
            with sp.Fori(0, B // PER - 1) as t:
                for u in range(PER):
                    n = t * PER + u
                    store(n, u)
                    sp.wait_ge(x1_stored, n * 16 + 16)
                    sp.wait_ge(s_done, n * 4 + 4)
                    load(n + PER, u)
            for n in range(B - PER, B):
                store(n, n % PER)
            sp.wait_ge(x1_stored, 16 * B)

        @block.gpsimd
        def _(pool):
            pool.dma_start(avg[:, :], group_avg).then_inc(consts_in, 16)
            for half in range(2):
                pool.dma_start(w1s[half * HALF:(half + 1) * HALF, :], w1).then_inc(consts_in, 16)
                pool.dma_start(bks[half * HALF:(half + 1) * HALF, :], bias_k).then_inc(consts_in, 16)
            pool.dma_start(b1s, b1.rearrange("(c a) -> c a", a=1)).then_inc(consts_in, 16)
            pool.dma_start(w2s, w2).then_inc(consts_in, 16)
            pool.dma_start(b2s, b2.rearrange("(a k) -> a k", a=1).to_broadcast([P, KE])).then_inc(consts_in, 16)
            pool.wait_ge(ex_zeroed, 1)
            for m, pi, po, kh in ((0, 0, 0, 1), (0, 0, 1, 0), (0, 1, 0, 2), (0, 1, 1, 1), (1, 0, 1, 2), (1, 1, 0, 0)):
                for k in range(KE):
                    pool.dma_start(ex[pi * HALF:(pi + 1) * HALF, k, 3 * m:3 * m + 3, po * C:(po + 1) * C],
                                   experts[:, k, kh, :, :]).then_inc(ex_in, 16)

            chain = Chain(pool, pool_step)

            def rstd(r, parity, c):
                pool.wait_ge(var_ready, r + 1)
                newton_rsqrt(nc.gpsimd, chain, affine[parity][:, 0, c], guess[:, c], var[:, c], three_halves[:, c], sq_pool[:, c], rstd_ready)

            def sample(t, k):
                n = t * PER + k
                for q in range(CH):
                    g, u = n * CH + q, q % 2
                    pool.wait_ge(hi_ready, g + 1)
                    nc.gpsimd.tensor_tensor(xz_lo[u][:, :, :, 1:W + 1], xn[:, u, :, :, :],
                                            xz_hi[u][:, :, :, 1:W + 1].bitcast(F32),
                                            ALU.subtract).then_inc(lo_ready, 1)
                    if q == 1:
                        rstd(n + 1, k % 2, cols(n))

            pool.wait_ge(set_up, 7)
            rstd(0, 1, INP)
            walk(pool, sample, chain, PER * NEWTON_STEPS)
            rstd(B + 1, 0, RES)

        @block.scalar
        def _(act):
            def normalise(t, k, q):
                n, u, x = t * PER + k, q % 2, raw[k % PER]
                scale, shift = affine[(k + 1) % 2][:, 0, INP], affine[(k + 1) % 2][:, 1, INP]
                ev, od = slice(0, HALF), slice(HALF, P)
                act.wait_ge(affine_ready, n + 1)
                wait_from(act, lo_ready, n * CH + (q - 1))
                parts = [(slice(0, P), 0, 0, q * CB, CB), (ev, 1, 0, q * CB + 1, CB), (od, 1, 0, q * CB - 1, CB)]
                if q == 0:
                    parts[2] = (od, 1, 1, 0, CB - 1)
                    nc.scalar.activation(xn[od, u, 1, 0, :], zeros[od, :], ACT.Identity).then_inc(xn_ready, 1)
                if q == CH - 1:
                    parts[1] = (ev, 1, 0, q * CB + 1, CB - 1)
                    nc.scalar.activation(xn[ev, u, 1, CB - 1, :], zeros[ev, :], ACT.Identity).then_inc(xn_ready, 1)
                for part, m, to, at, rows in parts:
                    nc.scalar.activation(xn[part, u, m, to:to + rows, :], x[part, at:at + rows, :], ACT.Identity,
                                         bias=shift[part, :], scale=scale[part, :]).then_inc(xn_ready, 1)

            def hidden(m):
                act.wait_ge(hid_done, m + 1)
                nc.scalar.activation(h, hid_ps, ACT.Relu, bias=b1s, scale=0.5).then_inc(h_ready, 1)

            def exps(m):
                act.wait_ge(logit_ready, m + 1)
                nc.scalar.activation(prob, logit, ACT.Exp, accum_out=total).then_inc(prob_ready, 1)

            def to_slot(n, u, parity, round_):
                act.wait_ge(affine_ready, round_ + 1)
                for pw in range(2):
                    dst, src, scale, shift = slot_move(n, u, parity, 1, pw)
                    nc.scalar.activation(dst, src, ACT.Identity, bias=shift, scale=scale).then_inc(s_done, 1)

            def sample(t, k):
                n = t * PER + k
                first, last = isinstance(n, int) and n == 0, isinstance(n, int) and n == B - 1
                for q in range(1, CH):
                    normalise(t, k, q)
                if not first:
                    to_slot(n - 1, (k - 1) % PER, k % 2, n + 1)
                if not last:
                    hidden(n + 1)
                    normalise(t, k + 1, 0)
                    exps(n + 1)

            act.wait_ge(set_up, 7)
            act.wait_ge(consts_in, 8 * 16)
            hidden(0)
            normalise(0, 0, 0)
            exps(0)
            walk(act, sample)
            to_slot(B - 1, (B - 1) % PER, 0, B + 1)

        @block.tensor
        def _(pe):
            def group(r, c):
                pe.wait_ge(me_ready, r + 1)
                nc.tensor.matmul(group_ps[:, c, :], avg[:, :], me[:, c, :], start=True, stop=True).then_inc(group_done, 1)

            def hid(m):
                pe.wait_ge(gmean_ready, m + 1)
                nc.tensor.matmul(hid_ps, w1s[:, :], gmean, start=True, stop=True).then_inc(hid_done, 1)

            def logits(m):
                pe.wait_ge(w2h_ready, m + 1)
                nc.tensor.matmul(logit_ps, ones[:, :], w2h, start=True, stop=True).then_inc(logit_done, 1)

            def sample(t, k):
                n = t * PER + k
                last = isinstance(n, int) and n == B - 1
                for q in range(CH):
                    g, u = n * CH + q, q % 2
                    pe.wait_ge(hi_ready, g + 1)
                    wait_from(pe, evac_done, g - 1)
                    if q == 0:
                        pe.wait_ge(w_ready, n + 1)
                    for m in range(2):
                        for dw in range(3):
                            for j, w in enumerate((w_hi, w_lo)):
                                nc.tensor.matmul(conv[u][:, :], w[:, 3 * m + dw, :], xz_hi[u][:, m, :, dw:dw + W],
                                                 start=(m == dw == j == 0), stop=False)
                        if m == 0 and q == 1:
                            group(n + 1, cols(n))
                        if m == 0 and q == 2 and not last:
                            hid(n + 1)
                        if m == 0 and q == 3 and not last:
                            logits(n + 1)
                    pe.wait_ge(lo_ready, g + 1)
                    for m in range(2):
                        for dw in range(3):
                            mm = nc.tensor.matmul(conv[u][:, :], w_hi[:, 3 * m + dw, :], xz_lo[u][:, m, :, dw:dw + W],
                                                  start=False, stop=(m == 1 and dw == 2))
                    mm.then_inc(conv_done, 1)

            pe.wait_ge(consts_in, 8 * 16)
            pe.wait_ge(set_up, 7)
            group(0, INP)
            hid(0)
            logits(0)
            walk(pe, sample)
            group(B + 1, RES)

        @block.vector
        def _(dve):
            chain = Chain(dve, dve_step)

            def input_stats(t, k):
                dve.wait_ge(raw_in[k % PER], t * 32 + 32 * (k // PER + 1))
                for q in range(CH):
                    nc.vector.bn_stats(bn[:, 1, q, :], chunk(raw[k % PER], q)).then_inc(dve_step, 1)
                    chain.count += 1
                dve.wait_ge(dve_step, chain.offset + chain.count)
                chain.carry(pause)
                chain.step(nc.vector.bn_aggr(mv[:, 1, :], bn[:, 1, :, :]))

            def result_stats():
                chain.carry(pause)
                chain.step(nc.vector.bn_aggr(mv[:, 0, :], bn[:, 0, :, :]))

            def squares(c):
                chain.step(nc.vector.tensor_tensor(sq[:, c], mv[:, c, 0], mv[:, c, 0], ALU.mult))
                nc.vector.tensor_copy(me[:, c, 0], mv[:, c, 0])
                nc.vector.tensor_tensor(me[:, c, 1], sq[:, c], mv[:, c, 1], ALU.add).then_inc(me_ready, 1)

            def group_var(r, c):
                dve.wait_ge(group_done, r + 1)
                chain.step(nc.vector.tensor_copy(gs[:, c, :], group_ps[:, c, :]))
                chain.step(nc.vector.tensor_tensor(sq[:, c], gs[:, c, 0], gs[:, c, 0], ALU.mult))
                chain.step(nc.vector.scalar_tensor_tensor(out=var[:, c], in0=gs[:, c, 1], scalar=GN_EPS, in1=sq[:, c],
                                                          op0=ALU.add, op1=ALU.subtract))
                rsqrt_guess(nc, chain, guess[:, c], sq[:, c], var[:, c]).then_inc(var_ready, 1)

            def group_affine(r, parity, c):
                dve.wait_ge(rstd_ready, r + 1)
                nc.vector.scalar_tensor_tensor(out=affine[parity][:, 1, c], in0=gs[:, c, 0], scalar=-1.0,
                                               in1=affine[parity][:, 0, c], op0=ALU.mult,
                                               op1=ALU.mult).then_inc(affine_ready, 1)
                dve.wait_ge(affine_ready, r + 1)

            def gate_mean(parity):
                nc.vector.tensor_scalar(gmean, mv[:, INP, 0], affine[parity][:, 0, INP], affine[parity][:, 1, INP],
                                        ALU.mult, ALU.add).then_inc(gmean_ready, 1)

            def to_slot(n, u, parity):
                for pw in range(2):
                    dst, src, scale, shift = slot_move(n, u, parity, 0, pw)
                    nc.vector.tensor_scalar(dst, src, scale, shift, ALU.mult, ALU.add).then_inc(s_done, 1)

            def gate_hidden(m):
                dve.wait_ge(h_ready, m + 1)
                nc.vector.tensor_scalar(w2h, w2s, h, None, ALU.mult).then_inc(w2h_ready, 1)

            def mix(m):
                dve.wait_ge(logit_done, m + 1)
                chain.step(nc.vector.tensor_tensor(logit, logit_ps, b2s, ALU.add))
                chain.step(nc.vector.reduce_max(top, logit, AX_X))
                nc.vector.tensor_scalar(logit, logit, top, None, ALU.subtract).then_inc(logit_ready, 1)
                dve.wait_ge(prob_ready, m + 1)
                chain.step(nc.vector.reciprocal(total, total))
                chain.step(nc.vector.tensor_scalar(alpha, prob, total, None, ALU.mult))
                chain.step(nc.vector.tensor_scalar(w_mix[:, :, :], ex[:, 0, :, :], alpha[:, 0:1], None, ALU.mult))
                for k in range(1, KE):
                    chain.step(nc.vector.scalar_tensor_tensor(out=w_mix[:, :, :], in0=ex[:, k, :, :],
                                                              scalar=alpha[:, k:k + 1], in1=w_mix[:, :, :],
                                                              op0=ALU.mult, op1=ALU.add))

            def split_weights():
                chain.step(nc.vector.tensor_copy(w_hi[:, :, :], w_mix[:, :, :]))
                nc.vector.tensor_tensor(w_lo[:, :, :], w_mix[:, :, :], w_hi[:, :, :].bitcast(F32),
                                        ALU.subtract).then_inc(w_ready, 1)

            def split_chunk(n, q):
                g, u = n * CH + q, q % 2
                dve.wait_ge(xn_ready, n * XN[-1] + XN[q])
                wait_from(dve, conv_done, g - 1)
                nc.vector.tensor_copy(xz_hi[u][:, :, :, 1:W + 1], xn[:, u, :, :, :]).then_inc(hi_ready, 1)

            def residual(g, u_raw, q):
                dve.wait_ge(conv_done, g + 1)
                x = chunk(raw[u_raw], q)
                nc.vector.scalar_tensor_tensor(out=x, in0=conv[q % 2][:, :], scalar=beff, in1=x,
                                               op0=ALU.add, op1=ALU.add).then_inc(evac_done, 1)
                dve.wait_ge(evac_done, g + 1)
                nc.vector.bn_stats(bn[:, 0, q, :], x).then_inc(dve_step, 1)
                chain.count += 1

            def effective_bias():
                chain.step(nc.vector.tensor_tensor(bprod, bks, alpha, ALU.mult))
                chain.step(nc.vector.reduce_sum(beff, bprod, AX_X))

            def sample(t, k):
                n = t * PER + k
                first, last = isinstance(n, int) and n == 0, isinstance(n, int) and n == B - 1
                for q in range(CH):
                    if q in (1, 3):
                        split_chunk(n, q)
                    if q == 0:
                        wait_from(dve, conv_done, n * CH)
                        split_weights()
                    if q != 2 and not (first and q == 0):
                        residual(n * CH + (q - 1), (k - (q == 0)) % PER, (q - 1) % CH)
                    if q == 0:
                        effective_bias()
                        if not first:
                            result_stats()
                        if not last:
                            input_stats(t, k + 1)
                        squares(cols(n))
                    if q == 1:
                        group_var(n + 1, cols(n))
                        split_chunk(n, 2)
                        residual(n * CH + 1, k % PER, 1)
                        group_affine(n + 1, k % 2, cols(n))
                        if not last:
                            gate_mean(k % 2)
                        if not first:
                            to_slot(n - 1, (k - 1) % PER, k % 2)
                    if q == 2 and not last:
                        gate_hidden(n + 1)
                    if q == 3 and not last:
                        split_chunk(n + 1, 0)
                        mix(n + 1)

            nc.vector.memset(ex[:, :, :, :], 0.0).then_inc(ex_zeroed, 1)
            for t in (*xz_hi, *xz_lo):
                nc.vector.memset(t[:, :, :, :].bitcast(F32), 0.0).then_inc(set_up, 1)
            nc.vector.memset(ones[:, :], 1.0).then_inc(set_up, 1)
            nc.vector.memset(zeros[:, :], 0.0)
            nc.vector.memset(three_halves, 1.5).then_inc(set_up, 1)
            nc.vector.memset(pause, 1.0).then_inc(set_up, 1)
            dve.wait_ge(set_up, 7)
            dve.wait_ge(consts_in, 8 * 16)
            input_stats(0, 0)
            squares(INP)
            group_var(0, INP)
            group_affine(0, 1, INP)
            gate_mean(1)
            gate_hidden(0)
            dve.wait_ge(ex_in, 6 * KE * 16)
            split_chunk(0, 0)
            mix(0)
            walk(dve, sample, chain, PER * PER_LOOP)
            residual(B * CH - 1, B % PER - 1, CH - 1)
            dve.wait_ge(dve_step, chain.count)
            result_stats()
            squares(RES)
            group_var(B + 1, RES)
            group_affine(B + 1, 0, RES)
            to_slot(B - 1, (B - 1) % PER, 0)


HEADS, HD = 8, 8
QR = 8
PE_TAPS = [(1, 1), (0, 1), (2, 1), (0, 0)]
DVE_TAPS = [(1, 0), (1, 2), (0, 2), (2, 0), (2, 2)]


def attention(nc, ctx, S, x1, x2, x3, consts, cos_k, sin_k, cos_q, sin_q, wqk, bqk, lepe_w, lepe_b):
    def sb(name, shape, dt=F32):
        return ctx.enter_context(nc.sbuf_tensor(f"at_{name}", shape, dt))

    sem = semaphores(nc, ctx, "at")

    xr = sb("xr", [P, J, W])
    G = sb("G", [P, J, W])
    T = sb("T", [P, J + 2, C])
    res = sb("res", [P, C, J])
    kt = [sb(f"kt{u}", [P, 8, W]) for u in range(2)]
    ke = [sb(f"ke{u}", [P, 8, W]) for u in range(2)]
    kcs0 = sb("kcs0", [P, 8, 2, W])
    lepe = [kcs0[:, 4 * u:4 * u + 4, :, :].rearrange("p i s w -> p (i s) w") for u in range(2)]
    tab_k = sb("tab_k", [P, 2, J, J])
    tab_q = sb("tab_q", [P, 2, J])
    qer = sb("qer", [P, 2, 2, QR, C])
    qe, qr = ([qer[:, u, i, :, :] for u in range(2)] for i in range(2))
    kcs = [kcs0[:, :, :, :], qer[:, 1].rearrange("p s h c -> p (s h c)").rearrange("p (i s w) -> p i s w", i=8, s=2)]
    qs = sb("qs", [P, QR, C])
    rzx = qs
    rz = sb("rz", [P, QR * C // P, 2 * HEADS])
    cst = sb("cst", [P, 6, P])
    avg, ident, mask, rot1, rot2, same_j = (cst[:, i, :] for i in range(6))
    wq = sb("wq", [P, P])
    wk = sb("wk", [P, P])
    diag = sb("diag", [P, len(PE_TAPS), P])
    ab = sb("ab", [P, W])
    kvw = sb("kvw", [P, 2, P])
    km = sb("km", [P, 2 * HEADS])
    bk = sb("bk", [P, W])
    ones = sb("ones", [P, 1])
    small = sb("small", [P, 64])
    lw, lb, bq, ks = small[:, 0:9], small[:, 9:10], small[:, 10:11], small[:, 11:12]
    stat = [small[:, 16 + 4 * i:20 + 4 * i].rearrange("p (a b) -> p a b", a=2) for i in range(3)]
    mv, me, gs = stat
    sq, var, guess, sq_pool = (small[:, 28 + 2 * i:30 + 2 * i] for i in range(4))
    three_halves, pause = small[:, 40:42], small[:, 42:43]
    affine = small[:, 36:40].rearrange("p (b a) -> p b a", b=2)
    bn = sb("bn", [P, 2, 4, 6])

    bank = lambda name: ctx.enter_context(nc.psum_tensor(f"at_ps_{name}", [P, 512], F32))
    tk_ps = [bank("tk0"), bank("tk1")]
    q_ps, zb_ps, out0, out1, ab_ps, tiny = (bank(x) for x in ("q", "zb", "out0", "out1", "ab", "tiny"))
    out_ps = [out0, out1]
    zt_ps = zb_ps[:, 0:64].rearrange("p (t h) -> p t h", h=2 * HEADS)
    group_ps, ksp_ps, ks_ps = tiny[:, 0:4].rearrange("p (a b) -> p a b", a=2), zb_ps[:, 0:1], tiny[:, 16:17]
    rot_ps = [tiny[:, 64:128], tiny[:, 128:192]]

    consts_in, set_up = sem("consts_in"), sem("set_up")
    x1_in, x2_ready, x2_stored, res_in, x3_stored = sem("x1_in"), sem("x2_ready"), sem("x2_stored"), sem("res_in"), [sem(f"x3_stored{q}") for q in range(2)]
    g_ready, tr_done, t_ready, k_done = sem("g_ready"), sem("tr_done"), sem("t_ready"), sem("k_done")
    kt_ready, ke_ready, kr_ready, kk_ready, kc_ready, ks_ready = (sem(x) for x in ("kt_ready", "ke_ready", "kr_ready", "kk_ready", "kc_ready", "ks_ready"))
    kv_done, ab_ready, rot_done, kvw_ready = sem("kv_done"), sem("ab_ready"), sem("rot_done"), sem("kvw_ready")
    q_done, qe_ready, qr_ready, qq_ready, qc_ready, qs_ready = (sem(x) for x in ("q_done", "qe_ready", "qr_ready", "qq_ready", "qc_ready", "qs_ready"))
    z_done, rz_ready, rzx_ready, zb_done, qz_ready = sem("z_done"), sem("rz_ready"), sem("rzx_ready"), sem("zb_done"), sem("qz_ready")
    lepe_done, out_done, lepe_ready, taps_done = sem("lepe_done"), sem("out_done"), sem("lepe_ready"), sem("taps_done")
    out_added, s_done, km_ready = sem("out_added"), sem("s_done"), sem("km_ready")
    me_ready, group_done, var_ready, rstd_ready, affine_ready = ([sem(f"{x}{i}") for i in range(2)] for x in ("me_ready", "group_done", "var_ready", "rstd_ready", "affine_ready"))
    dve_step, pool_step = sem("dve_step"), sem("pool_step")
    RES, INP = 0, 1
    lo, hi = slice(0, HALF), slice(HALF, P)

    def walk(eng, sample, chain=None, per_turn=0):
        sample(0)
        with eng.Fori(0, B - 2) as t:
            if chain:
                chain.turn(t, per_turn)
            sample(t + 1)
        if chain:
            chain.leave(B - 2)
        sample(B - 1)

    def pairs(ap):
        return ap.rearrange("p i (k e) -> p i k e", e=2)

    def table(which, b):
        return tab_k[:, which, b * 8:(b + 1) * 8, :].unsqueeze(3).to_broadcast([P, 8, J, 2])

    def angle(which, c):
        return tab_q[:, which, c * QR:(c + 1) * QR].unsqueeze(2).to_broadcast([P, QR, C])

    def bank_rows(ps):
        return ps[:, :].rearrange("p (h c) -> p h c", h=QR)

    def res_rows(c):
        return res[:, :, c * QR:(c + 1) * QR].rearrange("p c h -> p h c")

    def tap_views(t, c, out):
        kh, kw = t
        c0, c1 = (1 if kh == 0 else 0), (C - 1 if kh == 2 else C)
        return out[:, :, c0:c1], T[:, kw + c * QR:kw + (c + 1) * QR, c0 + kh - 1:c1 + kh - 1]

    def slot_move(m, g, pw):
        part = slice(g * HALF, (g + 1) * HALF)
        dst = S[pw * HALF:(pw + 1) * HALF, bass.ds(m * -1 + B, 1), :, g * 16:(g + 1) * 16].rearrange("p a h w -> p (a h) w")
        src = res[part, :, :].rearrange("p c (w q) -> p q c w", q=2)[:, pw]
        return dst, src, affine[part, 0, RES:RES + 1], affine[part, 1, RES:RES + 1]

    first = lambda m: isinstance(m, int) and m == 0
    last = lambda m: isinstance(m, int) and m == B - 1

    with nc.Block() as block:

        @block.sync
        def _(sp):
            def load_x1(m):
                sp.dma_start(xr[:, :, :].rearrange("p i w -> p (i w)"),
                             x1[bass.ds(m * -1 + (B - 1), 1), :, :].rearrange("a p f -> (a p) f")).then_inc(x1_in, 16)

            def halves(ap, m):
                return [ap[bass.ds(m * -1 + (B - 1), 1)].rearrange("a c h w -> (a c) h w")[:, :, g * J:(g + 1) * J] for g in range(2)]

            def store_x2(m):
                sp.wait_ge(x2_ready, m + 1)
                for half in range(2):
                    sp.dma_start(x2[bass.ds(m * -1 + (B - 1), 1)].rearrange("a c (i q) w -> (a c) q i w", q=2)[:, half],
                                 xr[half * HALF:(half + 1) * HALF, :, :]).then_inc(x2_stored, 16)

            load_x1(0)
            store_x2(0)

            def sample(m):
                before, after = m * 32, m + 1
                if not isinstance(m, int):
                    m = sp.snap(m)
                    before, after = sp.snap(m * 32), sp.snap(m + 1)
                if not last(m):
                    sp.wait_ge(g_ready, after)
                sp.wait_ge(x2_stored, before + 32)
                if not last(m):
                    load_x1(m + 1)
                if not first(m):
                    for q in range(2):
                        sp.wait_ge(x3_stored[q], before)
                    sp.wait_ge(s_done, before)
                for g, src in enumerate(halves(x2, m)):
                    sp.dma_start(res[g * HALF:(g + 1) * HALF, :, :], src).then_inc(res_in, 16)
                if not last(m):
                    store_x2(m + 1)
                sp.wait_ge(out_added, m * 4 + 4)
                for g in range(2):
                    for q in range(2):
                        dst = x3[bass.ds(m * -1 + (B - 1), 1), q * HALF:(q + 1) * HALF, :].rearrange(
                            "a p (i w) -> (a p) i w", i=J)[:, :, g * J:(g + 1) * J]
                        src = res[g * HALF:(g + 1) * HALF, :, :].rearrange("p (i q) w -> p q i w", q=2)[:, q]
                        sp.dma_start(dst, src).then_inc(x3_stored[q], 16)

            walk(sp, sample)
            for q in range(2):
                sp.wait_ge(x3_stored[q], 32 * B)

        @block.gpsimd
        def _(pool):
            chain = Chain(pool, pool_step)
            pool.dma_start(cst[:, :, :], consts).then_inc(consts_in, 16)
            for i, t in enumerate((cos_k, sin_k)):
                pool.dma_start(tab_k[:, i, :, :], t).then_inc(consts_in, 16)
            for i, t in enumerate((cos_q, sin_q)):
                pool.dma_start(tab_q[:, i, :], t).then_inc(consts_in, 16)
            pool.wait_ge(set_up, 2)
            for g in range(2):
                part = slice(g * HALF, (g + 1) * HALF)
                pool.dma_start(wq[part, part], wqk[:, 0:W]).then_inc(consts_in, 16)
                pool.dma_start(wk[part, part], wqk[:, W:2 * W]).then_inc(consts_in, 16)
                pool.dma_start(bq[part, :], bqk[0:W].rearrange("(c a) -> c a", a=1)).then_inc(consts_in, 16)
                pool.dma_start(lw[part, :], lepe_w).then_inc(consts_in, 16)
                pool.dma_start(lb[part, :], lepe_b.rearrange("(c a) -> c a", a=1)).then_inc(consts_in, 16)
            pool.dma_start(bk[:, :], bqk[W:2 * W].rearrange("(a k) -> a k", a=1).to_broadcast([P, W])).then_inc(consts_in, 16)

            def rstd(kind, r):
                pool.wait_ge(var_ready[kind], r + 1)
                c = slice(kind, kind + 1)
                newton_rsqrt(nc.gpsimd, chain, affine[:, 0, c], guess[:, c], var[:, c], three_halves[:, c], sq_pool[:, c], rstd_ready[kind])

            def to_result(m, c):
                if c == 0:
                    pool.wait_ge(res_in, m * 32 + 32)
                pool.wait_ge(lepe_ready, m * 4 + (c + 1))
                nc.gpsimd.tensor_tensor(res_rows(c), res_rows(c), lepe[c % 2], ALU.add).then_inc(out_added, 1)

            pool.wait_ge(consts_in, 16 * 16)
            pool.wait_ge(set_up, 6)
            rstd(INP, 0)

            def sample(m):
                for b in range(4):
                    pool.wait_ge(kk_ready, m * 4 + (b + 1))
                    wait_from(pool, kv_done, m * 4 + (b - 1))
                    if b == 0:
                        wait_from(pool, out_added, m * 4)
                    if b == 1:
                        wait_from(pool, out_done, m * 4)
                    nc.gpsimd.tensor_tensor(pairs(kcs[b % 2][:, :, 1, :]), pairs(kt[b % 2][:, :, :]), table(1, b),
                                            ALU.mult).then_inc(ks_ready, 1)
                    if b == 2 and not first(m):
                        rstd(RES, m - 1)
                for c in range(4):
                    g = m * 4 + c
                    if c >= 1:
                        to_result(m, c - 1)
                    pool.wait_ge(qz_ready, g + 1)
                    wait_from(pool, out_done, g)
                    nc.gpsimd.tensor_tensor(qs[:, :, :], qe[c % 2][:, :, :], angle(1, c), ALU.mult).then_inc(qs_ready, 1)
                    if c == 2 and not last(m):
                        rstd(INP, m + 1)
                to_result(m, 3)

            walk(pool, sample, chain, 2 * NEWTON_STEPS)
            rstd(RES, B - 1)

        @block.scalar
        def _(act):
            def normalise(m):
                act.wait_ge(affine_ready[INP], m + 1)
                wait_from(act, kv_done, m * 4)
                nc.scalar.activation(G[:, :, :].rearrange("p (i g) w -> p g i w", g=2),
                                     xr[:, :, :].rearrange("p (g i) w -> p g i w", g=2), ACT.Identity, bias=affine[:, 1, INP:INP + 1],
                                     scale=affine[:, 0, INP:INP + 1]).then_inc(g_ready, 1)

            def q_exp(m, c):
                g = m * 4 + c
                act.wait_ge(q_done, g + 1)
                if c == 1:
                    act.wait_ge(kv_done, m * 4 + 4)
                wait_from(act, qc_ready, g - 1)
                wait_from(act, qs_ready, g - 1)
                wait_from(act, out_done, g - 1)
                q = bank_rows(q_ps)
                nc.scalar.activation(qe[c % 2][:, :, :], q, ACT.Exp, bias=bq).then_inc(qe_ready, 1)
                nc.scalar.activation(qr[c % 2][:, :, :], q, ACT.Relu, bias=bq).then_inc(qr_ready, 1)

            def expand(m, c):
                g = m * 4 + c
                act.wait_ge(rz_ready, g + 1)
                wait_from(act, out_done, g)
                nc.scalar.activation(rzx[:, :, :].rearrange("p (t h) (k e) -> p t h k e", h=2, e=HD),
                                     rz[:, :, :].rearrange("p t (h k) -> p t h k", h=2).unsqueeze(4).to_broadcast([P, 4, 2, HEADS, HD]),
                                     ACT.Identity).then_inc(rzx_ready, 1)

            def sample(m):
                wait_from(act, q_done, m * 4)
                wait_from(act, lepe_done, m * 4)
                wait_from(act, taps_done, m * 4)
                for b in range(4):
                    act.wait_ge(tr_done, m * 4 + (b + 1))
                    nc.scalar.copy(T[:, 1 + 8 * b:9 + 8 * b, :], bank_rows(tk_ps[b % 2])).then_inc(t_ready, 1)
                act.wait_ge(t_ready, m * 6 + 4)
                nc.scalar.copy(T[hi, 0, :], T[lo, J, :]).then_inc(t_ready, 1)
                nc.scalar.copy(T[lo, J + 1, :], T[hi, 1, :]).then_inc(t_ready, 1)
                for b in range(4):
                    g = m * 4 + b
                    act.wait_ge(kt_ready, g + 1)
                    wait_from(act, kk_ready, g - 1)
                    nc.scalar.activation(ke[b % 2][:, :, :], kt[b % 2][:, :, :], ACT.Exp).then_inc(ke_ready, 1)
                    act.wait_ge(ke_ready, g + 1)
                    nc.scalar.activation(kt[b % 2][:, :, :], kt[b % 2][:, :, :], ACT.Relu).then_inc(kr_ready, 1)
                if not first(m):
                    act.wait_ge(affine_ready[RES], m)
                    for pw in range(2):
                        dst, src, scale, shift = slot_move(m - 1, 1, pw)
                        nc.scalar.activation(dst, src, ACT.Identity, bias=shift, scale=scale).then_inc(s_done, 8)
                q_exp(m, 0)
                for c in range(4):
                    expand(m, c)
                    if c < 3:
                        q_exp(m, c + 1)
                if not last(m):
                    normalise(m + 1)

            act.wait_ge(consts_in, 16 * 16)
            act.wait_ge(set_up, 6)
            normalise(0)
            walk(act, sample)
            act.wait_ge(affine_ready[RES], B)
            for pw in range(2):
                dst, src, scale, shift = slot_move(B - 1, 1, pw)
                nc.scalar.activation(dst, src, ACT.Identity, bias=shift, scale=scale).then_inc(s_done, 8)

        @block.tensor
        def _(pe):
            def group(kind, r):
                pe.wait_ge(me_ready[kind], r + 1)
                nc.tensor.matmul(group_ps[:, kind, :], avg, me[:, kind, :], start=True, stop=True).then_inc(group_done[kind], 1)

            def kv(m, b):
                g = m * 4 + b
                pe.wait_ge(kc_ready, g + 1)
                pe.wait_ge(ks_ready, g + 1)
                for i in range(4):
                    nc.tensor.matmul(ksp_ps, kt[b % 2][:, 2 * i:2 * i + 2, :], ones[:, :],
                                     start=(b == 0 and i == 0), stop=(b == 3 and i == 3))
                for i in range(8):
                    mm = nc.tensor.matmul(ab_ps[:, 0:W], kcs[b % 2][:, i, :, :], G[:, b * 8 + i, :],
                                          start=(b == 0 and i == 0), stop=(b == 3 and i == 7))
                mm.then_inc(kv_done, 1)

            def q_chunk(m, c):
                g = m * 4 + c
                wait_from(pe, qr_ready, g)
                nc.tensor.matmul(q_ps[:, :], wq[:, :], T[:, 1 + c * QR:1 + (c + 1) * QR, :],
                                 start=True, stop=True).then_inc(q_done, 1)

            def taps(m, c, which=range(len(PE_TAPS))):
                if which[0] == 0:
                    wait_from(pe, lepe_ready, m * 4 + (c - 1))
                for i in which:
                    out, x = tap_views(PE_TAPS[i], c, bank_rows(out_ps[c % 2]))
                    mm = nc.tensor.matmul(out, diag[:, i, :], x, start=(i == 0), stop=False)
                if i == len(PE_TAPS) - 1:
                    mm.then_inc(lepe_done, 1)

            def z_chunk(m, c):
                g = m * 4 + c
                if c == 0:
                    pe.wait_ge(km_ready, m + 1)
                pe.wait_ge(qq_ready, g + 1)
                wait_from(pe, rz_ready, g)
                tokens = qe[c % 2][:, :, :].rearrange("p (t h) c -> p t (h c)", h=2)
                for i in range(4):
                    mm = nc.tensor.matmul(zt_ps[:, i, :], tokens[:, i, :], km[:, :], start=True, stop=True)
                mm.then_inc(z_done, 1)

            def z_spread(m, c):
                g = m * 4 + c
                pe.wait_ge(rzx_ready, g + 1)
                wait_from(pe, qz_ready, g)
                for i in range(4):
                    mm = nc.tensor.transpose(zb_ps[:, i * P:(i + 1) * P], rzx[:, i * 2:i * 2 + 2, :], ident)
                mm.then_inc(zb_done, 1)

            def out_chunk(m, c):
                g = m * 4 + c
                if c == 0:
                    pe.wait_ge(kvw_ready, m * 2 + 2)
                pe.wait_ge(qc_ready, g + 1)
                pe.wait_ge(qs_ready, g + 1)
                nc.tensor.matmul(out_ps[c % 2][:, :], kvw[:, 0, :], qr[c % 2][:, :, :], start=False, stop=False)
                nc.tensor.matmul(out_ps[c % 2][:, :], kvw[:, 1, :], qs[:, :, :], start=False, stop=True).then_inc(out_done, 1)

            def turn_chunk(m, b):
                if b == 0:
                    pe.wait_ge(g_ready, m + 1)
                if b >= 2:
                    pe.wait_ge(t_ready, m * 6 + (b - 1))
                for i in range(4):
                    row = b * 8 + i * 2
                    mm = nc.tensor.transpose(tk_ps[b % 2][:, i * P:(i + 1) * P], G[:, row:row + 2, :], ident)
                mm.then_inc(tr_done, 1)

            def k_chunk(m, b):
                pe.wait_ge(t_ready, m * 6 + (3 + b if b < 2 else 4))
                if b >= 2:
                    pe.wait_ge(kt_ready, m * 4 + (b - 1))
                for i in range(4):
                    row = b * 8 + i * 2
                    mm = nc.tensor.matmul(tk_ps[b % 2][:, i * P:(i + 1) * P], T[:, 1 + row:3 + row, :], wk[:, :],
                                          start=True, stop=True)
                mm.then_inc(k_done, 1)

            def sample(m):
                turn_chunk(m, 2)
                turn_chunk(m, 3)
                k_chunk(m, 0)
                k_chunk(m, 1)
                pe.wait_ge(t_ready, m * 6 + 6)
                q_chunk(m, 0)
                k_chunk(m, 2)
                taps(m, 0)
                kv(m, 0)
                k_chunk(m, 3)
                if not first(m):
                    group(RES, m - 1)
                kv(m, 1)
                taps(m, 1, (0, 1, 2))
                kv(m, 2)
                kv(m, 3)
                taps(m, 1, (3,))
                pe.wait_ge(ab_ready, m + 1)
                nc.tensor.matmul(rot_ps[0], rot1, ab[:, :], start=True, stop=True)
                nc.tensor.matmul(rot_ps[1], rot2, ab[:, :], start=True, stop=True)
                nc.tensor.matmul(ks_ps, same_j, ks, start=True, stop=True).then_inc(rot_done, 1)
                for c in range(4):
                    z_chunk(m, c)
                    if c >= 1:
                        out_chunk(m, c - 1)
                    if c < 3:
                        q_chunk(m, c + 1)
                    if c == 2 and not last(m):
                        group(INP, m + 1)
                    z_spread(m, c)
                    if c in (1, 2):
                        taps(m, c + 1)
                if not last(m):
                    turn_chunk(m + 1, 0)
                    turn_chunk(m + 1, 1)
                out_chunk(m, 3)

            pe.wait_ge(consts_in, 16 * 16)
            pe.wait_ge(set_up, 6 + len(PE_TAPS))
            group(INP, 0)
            turn_chunk(0, 0)
            turn_chunk(0, 1)
            walk(pe, sample)
            group(RES, B - 1)

        @block.vector
        def _(dve):
            chain = Chain(dve, dve_step)

            def part_stats(kind, x, q):
                nc.vector.bn_stats(bn[:, kind, q, :], x).then_inc(dve_step, 1)
                chain.count += 1

            def stats(kind):
                dve.wait_ge(dve_step, chain.offset + chain.count)
                c = slice(kind, kind + 1)
                chain.carry(pause)
                chain.step(nc.vector.bn_aggr(mv[:, kind, :], bn[:, kind, :, :]))
                chain.step(nc.vector.tensor_tensor(sq[:, c], mv[:, c, 0], mv[:, c, 0], ALU.mult))
                nc.vector.tensor_copy(me[:, c, 0], mv[:, c, 0])
                nc.vector.tensor_tensor(me[:, c, 1], sq[:, c], mv[:, c, 1], ALU.add).then_inc(me_ready[kind], 1)

            def group_var(kind, r):
                c = slice(kind, kind + 1)
                dve.wait_ge(group_done[kind], r + 1)
                chain.step(nc.vector.tensor_copy(gs[:, c, :], group_ps[:, c, :]))
                chain.step(nc.vector.tensor_tensor(sq[:, c], gs[:, c, 0], gs[:, c, 0], ALU.mult))
                chain.step(nc.vector.scalar_tensor_tensor(out=var[:, c], in0=gs[:, c, 1], scalar=GN_EPS, in1=sq[:, c],
                                                          op0=ALU.add, op1=ALU.subtract))
                rsqrt_guess(nc, chain, guess[:, c], sq[:, c], var[:, c]).then_inc(var_ready[kind], 1)

            def group_affine(kind, r):
                c = slice(kind, kind + 1)
                dve.wait_ge(rstd_ready[kind], r + 1)
                nc.vector.scalar_tensor_tensor(out=affine[:, 1, c], in0=gs[:, c, 0], scalar=-1.0,
                                               in1=affine[:, 0, c], op0=ALU.mult, op1=ALU.mult).then_inc(affine_ready[kind], 1)

            def add_x1(m):
                dve.wait_ge(x1_in, m * 16 + 16)
                nc.vector.tensor_tensor(xr[:, :, :], xr[:, :, :],
                                        S[:, bass.ds(m * -1 + (B - 1), 1), :, :].rearrange("p a w i -> p i (a w)"),
                                        ALU.add).then_inc(x2_ready, 1)

            def input_stats(m, quarters):
                if quarters[0] == 0:
                    dve.wait_ge(x2_ready, m + 1)
                for q in quarters:
                    part_stats(INP, xr[:, q * 8:(q + 1) * 8, :].rearrange("p i w -> p (i w)"), q)

            def result_stats(m, quarters):
                if quarters[0] == 0:
                    dve.wait_ge(out_added, m * 4 + 4)
                for q in quarters:
                    part_stats(RES, res[:, q * 16:(q + 1) * 16, :].rearrange("p i w -> p (i w)"), q)

            def to_slot(m):
                group_affine(RES, m)
                dve.wait_ge(affine_ready[RES], m + 1)
                for pw in range(2):
                    dst, src, scale, shift = slot_move(m, 0, pw)
                    nc.vector.tensor_scalar(dst, src, scale, shift, ALU.mult, ALU.add).then_inc(s_done, 8)

            def k_bias(m, b):
                g = m * 4 + b
                dve.wait_ge(k_done, g + 1)
                wait_from(dve, kv_done, g - 1)
                nc.vector.tensor_tensor(kt[b % 2][:, :, :], tk_ps[b % 2][:, :].rearrange("p (i j) -> p i j", i=8),
                                        bk[:, :].unsqueeze(1).to_broadcast([P, 8, W]), ALU.add).then_inc(kt_ready, 1)

            def k_finish(m, b):
                g = m * 4 + b
                k = kt[b % 2]
                dve.wait_ge(kr_ready, g + 1)
                nc.vector.scalar_tensor_tensor(out=k[:, :, :], in0=ke[b % 2][:, :, :], scalar=1.0, in1=k[:, :, :],
                                               op0=ALU.min, op1=ALU.add).then_inc(kk_ready, 1)
                dve.wait_ge(kk_ready, g + 1)
                wait_from(dve, kv_done, g - 1)
                if b == 0:
                    wait_from(dve, out_added, m * 4)
                if b == 1:
                    wait_from(dve, out_done, m * 4)
                nc.vector.tensor_tensor(pairs(kcs[b % 2][:, :, 0, :]), pairs(k[:, :, :]), table(0, b), ALU.mult).then_inc(kc_ready, 1)

            def q_elu(m, c):
                g = m * 4 + c
                q = qe[c % 2]
                dve.wait_ge(qr_ready, g + 1)
                nc.vector.scalar_tensor_tensor(out=q[:, :, :], in0=q[:, :, :], scalar=1.0, in1=qr[c % 2][:, :, :],
                                               op0=ALU.min, op1=ALU.add).then_inc(qq_ready, 1)

            def normaliser(m, c):
                dve.wait_ge(z_done, m * 4 + (c + 1))
                chain.step(nc.vector.tensor_scalar(rz[:, :, :], zt_ps, 1e-6, None, ALU.add))
                nc.vector.reciprocal(rz[:, :, :], rz[:, :, :]).then_inc(rz_ready, 1)

            def q_scale(m, c):
                g = m * 4 + c
                q = qe[c % 2]
                dve.wait_ge(zb_done, g + 1)
                nc.vector.tensor_tensor(q[:, :, :], q[:, :, :], bank_rows(zb_ps), ALU.mult).then_inc(qz_ready, 1)
                dve.wait_ge(qz_ready, g + 1)
                nc.vector.tensor_tensor(qr[c % 2][:, :, :], q[:, :, :], angle(0, c), ALU.mult).then_inc(qc_ready, 1)

            def taps(m, c, which):
                for i in which:
                    t = DVE_TAPS[i]
                    out, x = tap_views(t, c, lepe[c % 2])
                    w = lw[:, 3 * t[0] + t[1]:3 * t[0] + t[1] + 1]
                    if i == 0:
                        wait_from(dve, out_added, m * 4 + (c - 1))
                        tap = nc.vector.tensor_scalar(out, x, w, lb, ALU.mult, ALU.add)
                    else:
                        tap = nc.vector.scalar_tensor_tensor(out=out, in0=x, scalar=w, in1=out, op0=ALU.mult, op1=ALU.add)
                    if i < len(DVE_TAPS) - 1:
                        chain.step(tap)
                    else:
                        tap.then_inc(taps_done, 1)

            def lepe_sum(m, c):
                g = m * 4 + c
                dve.wait_ge(taps_done, g + 1)
                dve.wait_ge(out_done, g + 1)
                nc.vector.tensor_tensor(lepe[c % 2], lepe[c % 2], bank_rows(out_ps[c % 2]), ALU.add).then_inc(lepe_ready, 1)

            def weights(m):
                dve.wait_ge(rot_done, m + 1)
                chain.step(nc.vector.tensor_copy(ks, ks_ps))
                nc.vector.tensor_scalar(km[:, :], mask[:, 0:P:HD], ks, None, ALU.mult).then_inc(km_ready, 1)
                for i in range(2):
                    nc.vector.tensor_tensor(kvw[:, i, :].rearrange("p (g e) -> p g e", g=2),
                                            rot_ps[i].unsqueeze(1).to_broadcast([P, 2, W]),
                                            mask.rearrange("p (g e) -> p g e", g=2), ALU.mult).then_inc(kvw_ready, 1)

            def sample(m):
                k_bias(m, 0)
                if not first(m):
                    result_stats(m - 1, (0, 1))
                k_bias(m, 1)
                k_finish(m, 0)
                if not first(m):
                    result_stats(m - 1, (2, 3))
                k_finish(m, 1)
                if not first(m):
                    stats(RES)
                k_bias(m, 2)
                if not first(m):
                    group_var(RES, m - 1)
                k_finish(m, 2)
                k_bias(m, 3)
                k_finish(m, 3)
                if not last(m):
                    add_x1(m + 1)
                if not first(m):
                    to_slot(m - 1)
                dve.wait_ge(kv_done, m * 4 + 4)
                chain.step(nc.vector.tensor_copy(ks, ksp_ps))
                nc.vector.tensor_copy(ab[:, :], ab_ps[:, 0:W]).then_inc(ab_ready, 1)
                for c in range(4):
                    q_elu(m, c)
                    taps(m, c, (0, 1))
                    if c == 0 and not last(m):
                        input_stats(m + 1, (0, 1))
                    if c == 0:
                        weights(m)
                    normaliser(m, c)
                    taps(m, c, (2,))
                    if c >= 1:
                        lepe_sum(m, c - 1)
                    if c == 2 and not last(m):
                        group_var(INP, m + 1)
                    if c == 3 and not last(m):
                        group_affine(INP, m + 1)
                    taps(m, c, (3, 4))
                    q_scale(m, c)
                    if c == 1 and not last(m):
                        input_stats(m + 1, (2, 3))
                        stats(INP)
                lepe_sum(m, 3)

            nc.vector.memset(wq[:, :], 0.0).then_inc(set_up, 1)
            nc.vector.memset(wk[:, :], 0.0).then_inc(set_up, 1)
            nc.vector.memset(T[:, :, :], 0.0).then_inc(set_up, 1)
            nc.vector.memset(ones[:, :], 1.0).then_inc(set_up, 1)
            nc.vector.memset(three_halves, 1.5).then_inc(set_up, 1)
            nc.vector.memset(pause, 1.0).then_inc(set_up, 1)
            dve.wait_ge(consts_in, 16 * 16)
            for i, t in enumerate(PE_TAPS):
                w = lw[:, 3 * t[0] + t[1]:3 * t[0] + t[1] + 1]
                nc.vector.tensor_scalar(diag[:, i, :], ident, w, None, ALU.mult).then_inc(set_up, 1)
            add_x1(0)
            input_stats(0, (0, 1, 2, 3))
            stats(INP)
            group_var(INP, 0)
            group_affine(INP, 0)
            walk(dve, sample, chain, AT_LOOP)
            result_stats(B - 1, (0, 1, 2, 3))
            stats(RES)
            group_var(RES, B - 1)
            to_slot(B - 1)


AT_LOOP = 46


def attention_constants():
    import numpy as np
    p = np.arange(P)
    j, g = p % HALF, p // HALF
    avg = (j[:, None] // 2 == j[None] // 2) * 0.25
    ident = np.eye(P)
    mask = (g[:, None] == g[None]) * (j[:, None] // HD == j[None] // HD) / float(H * W)
    rot1, rot2 = np.zeros((P, P)), np.zeros((P, P))
    for d in range(W):
        for out in (d, d + HALF):
            even = d % 2 == 0
            other = d + 1 if even else d - 1
            rot1[d, out] = 1
            rot1[HALF + other, out] = -1 if even else 1
            rot2[other, out] = 1 if even else -1
            rot2[HALF + d, out] = 1
    same_j = j[:, None] == j[None]
    mats = np.stack([avg, ident, mask, rot1, rot2, same_j], 1).astype(np.float32)
    theta = (1.0 / np.float32(10000.0) ** (np.arange(W // 2, dtype=np.float32) / np.float32(W // 2))).astype(np.float32)
    angles = np.arange(H, dtype=np.float32)[:, None] * theta
    i, gg = np.arange(J) // 2, np.arange(J) % 2
    h_k = 2 * (i + 16 * gg)[None, :] + g[:, None]
    h_q = 32 * g[:, None] + np.arange(J)[None, :]
    ak = angles[h_k]
    aq = angles[h_q, (j // 2)[:, None]]
    f = lambda a: np.ascontiguousarray(a.astype(np.float32))
    return f(mats), f(np.cos(ak)), f(np.sin(ak)), f(np.cos(aq)), f(np.sin(aq))


BUFS = 4


def x3_loads(nc, x3, x3_buf, loaded):
    with nc.Block() as block:
        @block.sync
        def _(sp):
            for n in range(BUFS):
                sp.dma_start(x3_buf[n][:, :, :].rearrange("p i w -> p (i w)"), x3[n]).then_inc(loaded[n], 16)


def final_sum(nc, ctx, S, x3, out, x3_buf, loaded):
    out_buf = [ctx.enter_context(nc.sbuf_tensor(f"fs_out{u}", [P, J, W], F32)) for u in range(BUFS)]
    sem = semaphores(nc, ctx, "fs")
    stored = [sem(f"stored{u}") for u in range(BUFS)]
    added = [sem(f"added_{e}") for e in ("dve", "pool")]
    PARTS = [[(0, 0), (1, 0), (0, 1)], [(1, 1)]]
    COUNT = 3

    def walk(eng, sample):
        for u in range(BUFS):
            sample(u, 0, u)
        with eng.Fori(0, B // BUFS - 1) as t:
            for u in range(BUFS):
                sample(t * BUFS + (u + BUFS), t + 1, u)

    def part_sum(which, eng, n, u, half, parity):
        rows = slice(half * 16, half * 16 + 16)
        src, dst = slice(parity * HALF, (parity + 1) * HALF), slice(half * HALF, (half + 1) * HALF)
        eng.tensor_tensor(out_buf[u][dst, :, :].rearrange("p (i q) w -> p q i w", q=2)[:, parity],
                          x3_buf[u][src, rows, :],
                          S[src, bass.ds(n, 1), :, rows].rearrange("p a w i -> p i (a w)"),
                          ALU.add).then_inc(added[which], COUNT // len(PARTS[which]))

    with nc.Block() as block:

        @block.sync
        def _(sp):
            with sp.Fori(0, B // BUFS - 1) as t:
                for u in range(BUFS):
                    n = t * BUFS + u
                    summed = sp.snap(n * COUNT + COUNT)
                    sp.wait_ge(added[0], summed)
                    sp.wait_ge(added[1], summed)
                    sp.dma_start(x3_buf[u][:, :, :].rearrange("p i w -> p (i w)"),
                                 x3[bass.ds(n + BUFS, 1)].rearrange("a p f -> (a p) f")).then_inc(loaded[u], 16)

        @block.scalar
        def _(act):
            with act.Fori(0, B // BUFS) as t:
                for u in range(BUFS):
                    n = t * BUFS + u
                    summed = act.snap(n * COUNT + COUNT)
                    act.wait_ge(added[0], summed)
                    act.wait_ge(added[1], summed)
                    for half in range(2):
                        act.dma_start(out[bass.ds(n, 1), :, half * J:(half + 1) * J, :].rearrange("a c h w -> (a c) (h w)"),
                                      out_buf[u][half * HALF:(half + 1) * HALF, :, :].rearrange("p h w -> p (h w)")
                                      ).then_inc(stored[u], 16)
            for u in range(BUFS):
                act.wait_ge(stored[u], 32 * (B // BUFS))

        @block.vector
        def _(dve):
            def sample(n, t, u):
                dve.wait_ge(loaded[u], t * 16 + 16)
                wait_from(dve, stored[u], t * 32)
                for half, parity in PARTS[0]:
                    part_sum(0, nc.vector, n, u, half, parity)

            walk(dve, sample)

        @block.gpsimd
        def _(pool):
            def sample(n, t, u):
                pool.wait_ge(loaded[u], t * 16 + 16)
                wait_from(pool, stored[u], t * 32)
                for half, parity in PARTS[1]:
                    part_sum(1, nc.gpsimd, n, u, half, parity)

            walk(pool, sample)


def build(nc, a, out):
    x1 = nc.dram_tensor("x1_scratch", [B, P, J * W], F32, kind="Internal").ap()
    x2 = nc.dram_tensor("x2_scratch", [B, C, H, W], F32, kind="Internal").ap()
    x3 = nc.dram_tensor("x3_scratch", [B, P, J * W], F32, kind="Internal").ap()
    with ExitStack() as whole:
        S = whole.enter_context(nc.sbuf_tensor("S", [P, B + 1, H, J], F32))

        def scnn(layer):
            for first, second, base in (("d", "u", 1), ("r", "l", 0)):
                with ExitStack() as ctx:
                    names = [f"L{layer}_conv_{{}}_{k}" for k in (first, second)]
                    sweep_pair(nc, ctx, S, base, [a[n.format("w")] for n in names], [a[n.format("b")] for n in names],
                               f"L{layer}{first}{second}")
                if base:
                    with ExitStack() as ctx:
                        relayout(nc, ctx, S, f"L{layer}re")

        with ExitStack() as ctx:
            dyn_conv(nc, ctx, S, a["x"], x1, a["L0_conv_experts"], a["L0_conv_bias"], a["L0_conv_w1"], a["L0_conv_b1"],
                     a["L0_conv_w2"], a["L0_conv_b2"], a["group_avg"])
        scnn(1)
        with ExitStack() as ctx:
            attention(nc, ctx, S, x1, x2, x3, a["matrices"], a["cos_k"], a["sin_k"], a["cos_q"], a["sin_q"],
                      a["L2_conv_qk_w"], a["L2_conv_qk_b"], a["L2_conv_lepe_w"], a["L2_conv_lepe_b"])
        x3_buf = [whole.enter_context(nc.sbuf_tensor(f"x3_buf{u}", [P, J, W], F32)) for u in range(BUFS)]
        loaded = [nc.alloc_semaphore(name=f"x3_loaded{u}") for u in range(BUFS)]
        x3_loads(nc, x3, x3_buf, loaded)
        scnn(3)
        with ExitStack() as ctx:
            final_sum(nc, ctx, S, x3, out, x3_buf, loaded)


def lay_out(inputs):
    import numpy as np
    a = {k: np.asarray(v) for k, v in inputs.items()}
    a["x"] = a["x"].reshape(B, C, J, 2, W)
    a["L0_conv_experts"] = a["L0_conv_experts"].transpose(2, 0, 3, 4, 1)
    for name in ("L0_conv_bias", "L0_conv_w1", "L0_conv_w2", "L2_conv_qk_w"):
        a[name] = a[name].T
    for layer in (1, 3):
        for k in "durl":
            a[f"L{layer}_conv_w_{k}"] = a[f"L{layer}_conv_w_{k}"].transpose(1, 2, 0)
    a["L2_conv_lepe_w"] = a["L2_conv_lepe_w"].reshape(C, 9)
    a["matrices"], a["cos_k"], a["sin_k"], a["cos_q"], a["sin_q"] = attention_constants()
    a["group_avg"] = a["matrices"][:, 0, :]
    return {k: np.ascontiguousarray(v) for k, v in a.items()}


def kernel(**inputs):
    import concourse.bacc as bacc
    from concourse.bass_utils import run_bass_kernel_spmd

    nc = bacc.Bacc("TRN2", target_bir_lowering=False, num_devices=1)
    arrays = lay_out(inputs)
    aps = {k: nc.dram_tensor(k, v.shape, mybir.dt.from_np(v.dtype), kind="ExternalInput").ap() for k, v in arrays.items()}
    out = nc.dram_tensor("out", [B, C, H, W], F32, kind="ExternalOutput").ap()
    build(nc, aps, out)
    result = run_bass_kernel_spmd(nc, [arrays], core_ids=[0])
    return result.results[0]["out"]
```
